# Optimizing a Trainium2 kernel written in Bass

```python
import numpy as np
import jax
import jax.numpy as jnp

def _softmax(x, axis=-1):
    return jax.nn.softmax(x, axis=axis)

def _gelu(x):
    return jax.nn.gelu(x, approximate=True)

def _silu(x):
    return jax.nn.silu(x)

def _sigmoid(x):
    return jax.nn.sigmoid(x)

def _layernorm(x, axis=-1, eps=1e-05):
    m = jnp.mean(x, axis=axis, keepdims=True)
    v = jnp.var(x, axis=axis, keepdims=True)
    return (x - m) / jnp.sqrt(v + eps)

def _scatter_add(tgt, idx, src, axis=0):
    return tgt.at[idx].add(src)

def _segment_sum(src, seg, n):
    return jax.ops.segment_sum(src, seg, n)
kernel_name = 'mk_flamingo_gated_d1_seqx_r4_35d3f4'

def setup_inputs(seed: int=0):
    np.random.seed(seed)
    _w = jnp.asarray

    def _rec_inputs():
        import jax
        import jax.numpy as jnp
        _rk = jax.random.key(seed)
        x = -0.0002928 + 1 * jax.random.normal(jax.random.fold_in(_rk, 1), (32, 128, 512), jnp.float32)
        _lenS = 128 - jax.random.randint(jax.random.fold_in(_rk, 7), (32,), 0, max(1, 128 // 4) + 1, jnp.int32)
        _lenS2 = 128 - jax.random.randint(jax.random.fold_in(_rk, 8), (32,), 0, max(1, 128 // 4) + 1, jnp.int32)
        _ctx_2048P = jax.random.normal(jax.random.fold_in(_rk, 11), (32, 16, 512), jnp.float32)
        _ctx_2048c = jax.random.dirichlet(jax.random.fold_in(_rk, 511), 0.3 * jnp.ones((16,), jnp.float32), (32, 128))
        _ctx_2048t = jnp.einsum('bsk,bkd->bsd', _ctx_2048c, _ctx_2048P)
        _ctx_2048t = _ctx_2048t * jax.lax.rsqrt(jnp.mean(jnp.square(_ctx_2048t)) + 1e-12) * 0.953939
        ctx_2048 = -1.39393e-06 + 0.999914 * (_ctx_2048t + 0.3 * jax.random.normal(jax.random.fold_in(_rk, 611), (32, 128, 512), jnp.float32))
        _g = jax.random.normal(jax.random.fold_in(_rk, 9001), (2, 1), jnp.float32)
        _g = jnp.sign(_g) * jnp.maximum(jnp.abs(_g), 1.0) + (_g == 0) * 1.0
        g_xattn = _g[0]
        g_ffn = _g[1]
        return (x, ctx_2048, g_xattn, g_ffn)
    x, ctx_2048, g_xattn, g_ffn = _rec_inputs()

    def _L0_xattn_setup():
        import jax, jax.numpy as jnp
        import numpy as np
        B, S, E, NH = (2, 256, 512, 16)
        DH = E // NH
        EPS = 1e-06

        def _mlstm_forward(q, k, v, Wi, bi, Wf, bf, ln_scale):
            b, s, e = q.shape
            nh = Wi.shape[1]
            dh = e // nh
            x = jnp.concatenate([q, k, v], axis=-1)
            ig = (x @ Wi + bi).transpose(0, 2, 1)[..., None]
            fg = (x @ Wf + bf).transpose(0, 2, 1)[..., None]
            split = lambda t: t.reshape(b, s, nh, dh).transpose(0, 2, 1, 3)
            qh, kh, vh = (split(q), split(k), split(v))
            log_f = jax.nn.log_sigmoid(fg)
            log_f_cum = jnp.concatenate([jnp.zeros((b, nh, 1, 1), q.dtype), jnp.cumsum(log_f, axis=2)], axis=2)
            fg_mat = log_f_cum - jnp.transpose(log_f_cum, (0, 1, 3, 2))
            ltr = jnp.tril(jnp.ones((s, s), dtype=bool))
            log_fg = jnp.where(ltr, fg_mat[:, :, 1:, 1:], -jnp.inf)
            log_D = log_fg + jnp.transpose(ig, (0, 1, 3, 2))
            max_log_D = jnp.max(log_D, axis=-1, keepdims=True)
            D = jnp.exp(log_D - max_log_D)
            qk = jnp.einsum('bhsd,bhtd->bhst', qh, kh) / jnp.sqrt(jnp.asarray(dh, q.dtype))
            C = qk * D
            normalizer = jnp.maximum(jnp.abs(C.sum(-1, keepdims=True)), jnp.exp(-max_log_D))
            Cn = C / (normalizer + EPS)
            h = jnp.einsum('bhst,bhtd->bhsd', Cn, vh)
            mu = h.mean(-1, keepdims=True)
            var = ((h - mu) ** 2).mean(-1, keepdims=True)
            hn = (h - mu) * jax.lax.rsqrt(var + EPS)
            hn = hn * ln_scale.reshape(1, nh, 1, dh)
            return hn.transpose(0, 2, 1, 3).reshape(b, s, e)
        key = jax.random.key(seed)
        ks = jax.random.split(key, 6)
        q = jax.random.normal(ks[0], (B, S, E), dtype=jnp.float32)
        k = jax.random.normal(ks[1], (B, S, E), dtype=jnp.float32)
        v = jax.random.normal(ks[2], (B, S, E), dtype=jnp.float32)
        Wi = jax.random.normal(ks[3], (3 * E, NH), dtype=jnp.float32) * 0.02
        bi = jax.random.normal(ks[4], (NH,), dtype=jnp.float32) * 0.1
        Wf = jax.random.normal(ks[5], (3 * E, NH), dtype=jnp.float32) * 0.02
        bf = jnp.linspace(3.0, 6.0, NH, dtype=jnp.float32)
        ln_scale = jnp.ones((E,), dtype=jnp.float32)
        return {'q': q, 'k': k, 'v': v, 'Wi': Wi, 'bi': bi, 'Wf': Wf, 'bf': bf, 'ln_scale': ln_scale}
    _L0_xattn_all = _L0_xattn_setup()
    _L0_xattn_in = {k: v for k, v in _L0_xattn_all.items() if k in ('Wi', 'bi', 'Wf', 'bf', 'ln_scale')}
    del _L0_xattn_all

    def _L0_ffn_setup():
        import jax, jax.numpy as jnp
        import numpy as np
        E, R, K = (8, 8, 2)
        D, F = (512, 2048)
        B, S = (2, 512)
        SCALING = 16.0 / 8.0

        def act(x):
            return jax.nn.gelu(x, approximate=True)
        key = jax.random.key(seed)
        ks = jax.random.split(key, 12)
        return {'hidden_states': jax.random.normal(ks[0], (B, S, D), jnp.float32), 'W_r': jax.random.normal(ks[1], (E, D), jnp.float32) * 0.02, 'b_r': jnp.zeros((E,), jnp.float32), 'W1': jax.random.normal(ks[2], (F, D), jnp.float32) * 0.02, 'b1': jnp.zeros((F,), jnp.float32), 'W2': jax.random.normal(ks[3], (D, F), jnp.float32) * 0.02, 'b2': jnp.zeros((D,), jnp.float32), 'A1': jax.random.normal(ks[4], (E, R, D), jnp.float32) * 0.02, 'B1': jax.random.normal(ks[5], (F, R) * 1 + ()).reshape(1, F, R).repeat(1, 0) * 0.0 + jax.random.normal(ks[5], (E, F, R), jnp.float32) * 0.02, 'A2': jax.random.normal(ks[6], (E, R, F), jnp.float32) * 0.02, 'B2': jax.random.normal(ks[7], (E, D, R), jnp.float32) * 0.02}
    _L0_ffn_all = _L0_ffn_setup()
    _L0_ffn_in = {k: v for k, v in _L0_ffn_all.items() if k in ('W_r', 'b_r', 'W1', 'b1', 'W2', 'b2', 'A1', 'B1', 'A2', 'B2')}
    del _L0_ffn_all
    return {'x': x, 'ctx_2048': ctx_2048, 'g_xattn': g_xattn, 'g_ffn': g_ffn, 'L0_xattn_Wi': _L0_xattn_in['Wi'], 'L0_xattn_bi': _L0_xattn_in['bi'], 'L0_xattn_Wf': _L0_xattn_in['Wf'], 'L0_xattn_bf': _L0_xattn_in['bf'], 'L0_xattn_ln_scale': _L0_xattn_in['ln_scale'], 'L0_ffn_W_r': _L0_ffn_in['W_r'], 'L0_ffn_b_r': _L0_ffn_in['b_r'], 'L0_ffn_W1': _L0_ffn_in['W1'], 'L0_ffn_b1': _L0_ffn_in['b1'], 'L0_ffn_W2': _L0_ffn_in['W2'], 'L0_ffn_b2': _L0_ffn_in['b2'], 'L0_ffn_A1': _L0_ffn_in['A1'], 'L0_ffn_B1': _L0_ffn_in['B1'], 'L0_ffn_A2': _L0_ffn_in['A2'], 'L0_ffn_B2': _L0_ffn_in['B2']}

def reference(x, ctx_2048, g_xattn, g_ffn, L0_xattn_Wi, L0_xattn_bi, L0_xattn_Wf, L0_xattn_bf, L0_xattn_ln_scale, L0_ffn_W_r, L0_ffn_b_r, L0_ffn_W1, L0_ffn_b1, L0_ffn_W2, L0_ffn_b2, L0_ffn_A1, L0_ffn_B1, L0_ffn_A2, L0_ffn_B2):
    import jax
    import jax.numpy as jnp

    def _L0_xattn_ref(q, k, v, Wi, bi, Wf, bf, ln_scale):
        import jax, jax.numpy as jnp
        import numpy as np
        B, S, E, NH = (2, 256, 512, 16)
        DH = E // NH
        EPS = 1e-06

        def _mlstm_forward(q, k, v, Wi, bi, Wf, bf, ln_scale):
            b, s, e = q.shape
            nh = Wi.shape[1]
            dh = e // nh
            x = jnp.concatenate([q, k, v], axis=-1)
            ig = (x @ Wi + bi).transpose(0, 2, 1)[..., None]
            fg = (x @ Wf + bf).transpose(0, 2, 1)[..., None]
            split = lambda t: t.reshape(b, s, nh, dh).transpose(0, 2, 1, 3)
            qh, kh, vh = (split(q), split(k), split(v))
            log_f = jax.nn.log_sigmoid(fg)
            log_f_cum = jnp.concatenate([jnp.zeros((b, nh, 1, 1), q.dtype), jnp.cumsum(log_f, axis=2)], axis=2)
            fg_mat = log_f_cum - jnp.transpose(log_f_cum, (0, 1, 3, 2))
            ltr = jnp.tril(jnp.ones((s, s), dtype=bool))
            log_fg = jnp.where(ltr, fg_mat[:, :, 1:, 1:], -jnp.inf)
            log_D = log_fg + jnp.transpose(ig, (0, 1, 3, 2))
            max_log_D = jnp.max(log_D, axis=-1, keepdims=True)
            D = jnp.exp(log_D - max_log_D)
            qk = jnp.einsum('bhsd,bhtd->bhst', qh, kh) / jnp.sqrt(jnp.asarray(dh, q.dtype))
            C = qk * D
            normalizer = jnp.maximum(jnp.abs(C.sum(-1, keepdims=True)), jnp.exp(-max_log_D))
            Cn = C / (normalizer + EPS)
            h = jnp.einsum('bhst,bhtd->bhsd', Cn, vh)
            mu = h.mean(-1, keepdims=True)
            var = ((h - mu) ** 2).mean(-1, keepdims=True)
            hn = (h - mu) * jax.lax.rsqrt(var + EPS)
            hn = hn * ln_scale.reshape(1, nh, 1, dh)
            return hn.transpose(0, 2, 1, 3).reshape(b, s, e)
        return _mlstm_forward(q, k, v, Wi, bi, Wf, bf, ln_scale)

    def _L0_ffn_ref(hidden_states, W_r, b_r, W1, b1, W2, b2, A1, B1, A2, B2):
        import jax, jax.numpy as jnp
        import numpy as np
        E, R, K = (8, 8, 2)
        D, F = (512, 2048)
        B, S = (2, 512)
        SCALING = 16.0 / 8.0

        def act(x):
            return jax.nn.gelu(x, approximate=True)
        b, s, d = hidden_states.shape
        N = b * s
        x = hidden_states.reshape(N, d)
        probs = jax.nn.softmax(x @ W_r.T + b_r, axis=-1)
        w_topk, idx_topk = jax.lax.top_k(probs, K)
        base1 = x @ W1.T + b1
        u1 = jnp.einsum('nd,erd->ner', x, A1)
        B1_rf = B1.transpose(0, 2, 1).reshape(E * R, F)
        B2_rf = B2.transpose(0, 2, 1).reshape(E * R, d)
        res = jnp.zeros((N, d), hidden_states.dtype)
        for k in range(K):
            oh = jax.nn.one_hot(idx_topk[:, k], E, dtype=x.dtype)
            z1 = (u1 * oh[:, :, None]).reshape(N, E * R)
            h = act(base1 + z1 @ B1_rf * SCALING)
            u2 = jnp.einsum('nf,erf->ner', h, A2)
            z2 = (u2 * oh[:, :, None]).reshape(N, E * R)
            y = h @ W2.T + b2 + z2 @ B2_rf * SCALING
            res = res + w_topk[:, k:k + 1] * y
        return res.reshape(b, s, d)
    x = x + jnp.tanh(g_xattn[0]) * _L0_xattn_ref(_layernorm(x, axis=-1), ctx_2048, ctx_2048, L0_xattn_Wi, L0_xattn_bi, L0_xattn_Wf, L0_xattn_bf, L0_xattn_ln_scale)
    x = x + jnp.tanh(g_ffn[0]) * _L0_ffn_ref(_layernorm(x, axis=-1), L0_ffn_W_r, L0_ffn_b_r, L0_ffn_W1, L0_ffn_b1, L0_ffn_W2, L0_ffn_b2, L0_ffn_A1, L0_ffn_B1, L0_ffn_A2, L0_ffn_B2)
    return x

_drawn_inputs = setup_inputs


def setup_inputs(seed=0):
    import zlib

    import numpy as np

    out = dict(_drawn_inputs(seed))
    spreads = {'L0_xattn_ln_scale': (1.0, 0.2),
     'L0_ffn_b_r': (0.0, 0.8),
     'L0_ffn_b1': (0.0, 0.605),
     'L0_ffn_b2': (0.0, 1.107)}
    factors = {'L0_xattn_bi': 64.0,
     'L0_ffn_W_r': 5.323,
     'L0_ffn_A1': 8.0,
     'L0_ffn_B1': 8.0,
     'L0_ffn_A2': 8.0,
     'L0_ffn_B2': 8.0}
    for name, (base, spread) in spreads.items():
        noise = np.random.default_rng([zlib.crc32(name.encode()), seed]).standard_normal(out[name].shape)
        drawn = base * np.exp(spread * noise) if base else spread * noise
        out[name] = jnp.asarray(drawn.astype(out[name].dtype))
    for name, factor in factors.items():
        out[name] = (out[name] * factor).astype(out[name].dtype)
    return out
```

```python
from contextlib import ExitStack

import concourse.bass as bass
from concourse import mybir

F32 = mybir.dt.float32
F16 = mybir.dt.float16
ALU = mybir.AluOpType
ACT = mybir.ActivationFunctionType
AX = mybir.AxisListType.X

P = 128
WS = 64.0
LORA = 2.0
EPS_LN = 1e-5
EPS = 1e-6


class Count:

    def __init__(self, sem, per):
        self.sem, self.per = sem, per

    def at(self, n, k):
        return n * self.per + k


def past(n):
    return not isinstance(n, int) or n >= 0


def apart(eng, n, passed):
    if not isinstance(n, int):
        eng.sem_inc(passed.sem)


def flamingo_kernel(nc, x, ctx_tok, ctx_T, gx, gf, wgate, bgate, lnscale, w1t, w2t, b1c, b2, a1r, br, b1lo, a2t, b2lo,
                    out):
    NB, S, D = x.shape
    NP = NB // 2
    DC = D // P
    NH = wgate.shape[2] // 2
    DH = D // NH
    FF = w1t.shape[1]
    FC = FF // P
    NS = FC // 2
    NE = br.shape[0]
    R64 = b1lo.shape[0]
    RK = R64 // NE
    T = 2 * S
    HB = 2 * NH
    NR = 8
    SC = float(DH) ** -0.5
    AC = R64 + NE
    assert S == P and NS == 8 and NH == 16 and DH == 32 and T * 2 == 512

    x_d = x.rearrange("(n b) s d -> n s b d", b=2)
    v_d = ctx_tok.rearrange("(n b) s d -> n s b d", b=2)
    k_d = ctx_T.rearrange("n (c p) t -> n p c t", p=P)
    o_d = out.rearrange("(n b) s d -> n s b d", b=2)

    with ExitStack() as ctx:
        def sb(name, shape, dt=F32):
            return ctx.enter_context(nc.sbuf_tensor(name, shape, dt))

        def cnt(name, per):
            return Count(ctx.enter_context(nc.semaphore(name)), per)

        Y = [ctx.enter_context(nc.psum_tensor(f"y{b}", [P, D], F32)) for b in range(2)]
        U = ctx.enter_context(nc.psum_tensor("u_lora", [P, 512], F32))
        H = [ctx.enter_context(nc.psum_tensor(f"hid{b}", [P, 512], F32)) for b in range(2)]
        R = [ctx.enter_context(nc.psum_tensor(f"ring{b}", [P, 512], F32)) for b in range(2)]
        G = ctx.enter_context(nc.psum_tensor("gates_av", [P, 512], F32))

        w1 = [sb(f"w1_{i}", [P, DC, FF], F16) for i in "hl"]
        w2 = [sb(f"w2_{i}", [P, FC, D], F16) for i in "hl"]
        b1w = [sb(f"b1w_{i}", [P, FF], F16) for i in "hl"]
        a2 = [sb(f"a2_{i}", [P, FC, R64], F16) for i in "hl"]
        a1 = [sb(f"a1_{i}", [P, DC, AC], F16) for i in "hl"]
        b2w = [sb(f"b2w_{i}", [P, D], F16) for i in "hl"]
        wg = sb("wg", [P, 3 * DC, 2 * NH])
        b1s = sb("b1s", [P, FC])
        bg = sb("bg", [P, 4 * NH])
        lnsg = sb("lnsg", [P, D])
        b2g = sb("b2g", [P, D])
        brb = sb("brb", [P, 2, NE])
        tg = sb("tg", [P, 4])
        ident = sb("ident", [P, P])
        identh = sb("identh", [P, P], F16)
        tri = sb("tri", [P, P])
        ntri = sb("ntri", [P, P])
        rev = sb("rev", [P, 2, NE])
        mhalf = sb("mhalf", [P, HB])
        xin = sb("xin", [P, 2, D])
        xres = sb("xres", [P, 2, D])
        kin = sb("kin", [P, DC, T])
        kT = sb("kT", [P, DC, T])
        vin = sb("vin", [P, 2, D])
        vaug = sb("vaug", [P, 2, NH, DH + 1])
        qn = sb("qn", [P, 2, D])
        qT = sb("qT", [P, DC, 2, P])
        gb = sb("gb", [P, 4 * NH])
        gt = sb("gt", [P, 4, HB])
        aT = sb("aT", [HB, P])
        MT = sb("MT", [HB, P])
        FM = sb("FM", [HB, P])
        em = sb("em", [HB, P])
        emt = sb("emt", [P, HB])
        acol = sb("acol", [P, HB])
        decay = sb("decay", [P, 2, NH, P])
        Ct = sb("Ct", [P, 3, 4, P])
        u = sb("u", [P, HB, DH + 1])
        uc = sb("uc", [P, 2, D])
        st = sb("st", [P, 8, HB])
        bn = sb("bn", [P, 2, 2, 8])
        rv = sb("rv", [P, 2, 2, 2])
        x1 = sb("x1", [P, 2, D])
        xT = [sb(f"xT_{i}", [P, DC, T], F16) for i in "hl"]
        lg = sb("lg", [P, 2, NE])
        l2 = sb("l2", [P, 2, NE])
        eq = sb("eq", [P, 2, NE])
        mx = sb("mx", [P, 6, 2])
        ex = sb("ex", [P, 2 * NE + 2])
        pe_ = sb("pe_", [P, 2 * NE + 2])
        rt = sb("rt", [P, 2 + 4 * NE])
        rtk = sb("rtk", [P, 2 + 4 * NE])
        ohd = sb("ohd", [P, 2, NE])
        c2 = sb("c2", [P, 2])
        u1s = sb("u1s", [P, 2 * NE, RK])
        zf = sb("zf", [P, 2, 2 * NE, RK])
        zsp = sb("zsp", [P, 4, 2, R64], F16)
        zs = sb("zs", [P, 2, T], F16)
        rb = sb("rb", [P, T])
        hid = sb("hid01", [P, 2, 2, 512])
        gv = [sb(f"gv_{i}", [P, 2, 2, 512], F16) for i in "hl"]
        uv = sb("uv", [P, 4, 2 * NE, RK])
        z2sp = sb("z2sp", [P, 2, 2, R64], F16)
        z2s = sb("z2s", [P, 2, P], F16)
        xoo = sb("xoo", [P, 4, D])
        mscr = nc.dram_tensor("mscr", (HB, P), F32, kind="Internal").ap()
        stage = [hid[:, :, :, :].rearrange("p a b c -> p (a b c)"), xoo[:, :, :].rearrange("p a b -> p (a b)")]

        ld_c = cnt("ld_c", 0)
        ld_x, ld_k, ld_v = cnt("ld_x", 16), cnt("ld_k", 16), cnt("ld_v", 16)
        ld_w = [cnt(f"ld_w{i}", 0) for i in range(2)]
        m_wr, m_bc, st_o = cnt("m_wr", 16), cnt("m_bc", 16), cnt("st_o", 16)
        passed = cnt("passed", 0)
        c_pool, c_dve, c_act = cnt("c_pool", 0), cnt("c_dve", 0), cnt("c_act", 0)
        w_hi, w_lo = cnt("w_hi", 0), cnt("w_lo", 0)
        cp_x, cp_k, cp_v = cnt("cp_x", 1), cnt("cp_k", 1), cnt("cp_v", 1)
        ln1, rs1, q_nd = cnt("ln1", 3), cnt("rs1", 2), cnt("q_nd", 2)
        qt_p, qt_s = cnt("qt_p", 2), cnt("qt_s", 2)
        gat_p, gat_s, gat_e, lf_d, lf_p = cnt("gat_p", 1), cnt("gat_s", 2), cnt("gat_e", 2), cnt("lf_d", 1), cnt("lf_p", 1)
        mx_d = cnt("mx_d", 4)
        em_a, em_p, em_s = cnt("em_a", 1), cnt("em_p", 1), cnt("em_s", 1)
        arg_g, dec_a, dec_g = cnt("arg_g", 4), cnt("dec_a", 4), cnt("dec_g", 4)
        qk_p, c_d, av_p, av_s = cnt("qk_p", 8), cnt("c_d", 8), cnt("av_p", 4), cnt("av_s", 4)
        po_d, po_a, po_g = cnt("po_d", 7), cnt("po_a", 2), cnt("po_g", 3)
        ln2, rs2, xn_d = cnt("ln2", 3), cnt("rs2", 2), cnt("xn_d", 2)
        xt_p, xt_h, xt_l = cnt("xt_p", 2), cnt("xt_h", 2), cnt("xt_l", 2)
        ro_p, ro_d, ro_e, z_p, z_s = cnt("ro_p", 1), cnt("ro_d", 25), cnt("ro_e", 1), cnt("z_p", 1), cnt("z_s", 2)
        base_p, g0_a, del_p, g1_a = cnt("base_p", NS), cnt("g0_a", 2 * NS), cnt("del_p", NS), cnt("g1_a", 2 * NS)
        v_d_, g_d_, hi_a, lo_d = cnt("v_d", NS), cnt("g_d", NS), cnt("hi_a", 2 * NS), cnt("lo_d", 2 * NS)
        w2_p = cnt("w2_p", NS)
        z2_d, z2_p, z2_s, y_p, y_d = cnt("z2_d", 7), cnt("z2_p", 1), cnt("z2_s", 1), cnt("y_p", 1), cnt("y_d", 2)
        xo_d = cnt("xo_d", 3)

        block = ctx.enter_context(nc.Block())
        NCONST = 9
        jobs = []
        for c in range(DC):
            jobs.append(([(w1t[c * P:(c + 1) * P, :], 0, P, 0, FF)], [(0, FF, WS, [w[:, c, :] for w in w1])]))
        for c in range(4):
            n = FC // 4
            src = w2t[c * n * P:(c + 1) * n * P, :].rearrange("(k p) d -> p k d", p=P)
            jobs.append(([(src, 0, P, 0, n * D)],
                         [(0, n * D, WS, [w[:, c * n:(c + 1) * n, :].rearrange("p k d -> p (k d)") for w in w2])]))
        jobs.append(([(b1lo, 0, R64, 0, FF), (b1lo, R64, P, 0, FF)], [(0, FF, WS * LORA, [w[:, :] for w in b1w])]))
        o1 = FC * R64
        o2 = o1 + DC * AC
        jobs.append(([(a2t.rearrange("(k p) r -> p k r", p=P), 0, P, 0, o1),
                      (a1r.rearrange("(c p) r -> p c r", p=P), 0, P, o1, o2),
                      (b2lo, 0, R64, o2, o2 + D), (b2lo, R64, P, o2, o2 + D)],
                     [(0, o1, WS, [w[:, :, :].rearrange("p k r -> p (k r)") for w in a2]),
                      (o1, o2, WS, [w[:, :, :].rearrange("p k r -> p (k r)") for w in a1]),
                      (o2, o2 + D, WS * LORA, [w[:, :] for w in b2w])]))
        parts = [len(job[1]) for job in jobs]

        def bc2(ap):
            return ap.unsqueeze(1).to_broadcast([P, 2, ap.shape[1]])

        def unit(j):
            return decay[:, j // 2, 8 * (j % 2):8 * (j % 2) + 8, :]

        def steps(eng, body):
            body(-2)
            body(-1)
            body(0)
            with eng.Fori(1, NP - 2) as t:
                body(t)
            body(NP - 2)
            body(NP - 1)
            body(NP)

        def ok(n):
            return not isinstance(n, int) or 0 <= n < NP

        @block.sync
        def _(sp):
            def load(n):
                if past(n - 1):
                    sp.wait_ge(cp_x.sem, cp_x.at(n - 1, 1))
                if past(n - 1):
                    sp.wait_ge(q_nd.sem, q_nd.at(n - 1, 2))
                sp.dma_start(xin[:, :, :], x_d[n]).then_inc(ld_x.sem, 16)
                if past(n - 1):
                    sp.wait_ge(cp_k.sem, cp_k.at(n - 1, 1))
                if past(n - 1):
                    sp.wait_ge(gat_p.sem, gat_p.at(n - 1, 1))
                sp.dma_start(kin[:, :, :], k_d[n]).then_inc(ld_k.sem, 16)
                if past(n - 1):
                    sp.wait_ge(cp_v.sem, cp_v.at(n - 1, 1))
                sp.dma_start(vin[:, :, :], v_d[n]).then_inc(ld_v.sem, 16)

            def weights(j):
                if j >= 2:
                    sp.wait_ge(w_hi.sem, sum(parts[:j - 1]))
                    sp.wait_ge(w_lo.sem, sum(parts[:j - 1]))
                for src, p0, p1, c0, c1_ in jobs[j][0]:
                    dst = stage[j % 2][p0:p1, c0:c1_]
                    if len(src.shape) == 3:
                        dst = dst.rearrange("p (a b) -> p a b", b=src.shape[2])
                    sp.dma_start(dst, src).then_inc(ld_w[j % 2].sem, 16)

            def body(t):
                u_, m, p = t - 1, t + 1, t + 2
                if isinstance(t, int) and t == -2:
                    load(0)
                    sp.dma_start(wg[:, :, :], wgate).then_inc(ld_c.sem, 16)
                    sp.dma_start(bg[:, :], bgate.partition_broadcast(P)).then_inc(ld_c.sem, 16)
                    sp.dma_start(tg[:, 0:1], gx.partition_broadcast(P)).then_inc(ld_c.sem, 16)
                    sp.dma_start(tg[:, 1:2], gf.partition_broadcast(P)).then_inc(ld_c.sem, 16)
                    sp.dma_start(lnsg[:, :], lnscale.partition_broadcast(P)).then_inc(ld_c.sem, 16)
                    sp.dma_start(b2g[:, :], b2.partition_broadcast(P)).then_inc(ld_c.sem, 16)
                    sp.dma_start(brb[:, 0, :], br.partition_broadcast(P)).then_inc(ld_c.sem, 16)
                    sp.dma_start(brb[:, 1, :], br.partition_broadcast(P)).then_inc(ld_c.sem, 16)
                    sp.dma_start(b1s[:, :], b1c).then_inc(ld_c.sem, 16)
                    weights(0)
                    weights(1)
                    return
                if ok(m):
                    sp.wait_ge(mx_d.sem, mx_d.at(m, 3))
                    if past(m - 1):
                        sp.wait_ge(m_bc.sem, m_bc.at(m - 1, 16))
                    sp.dma_start(mscr, MT[:, :]).then_inc(m_wr.sem, 16)
                    sp.wait_ge(m_wr.sem, m_wr.at(m, 16))
                    if past(m - 1):
                        sp.wait_ge(c_d.sem, c_d.at(m - 1, 8))
                    sp.dma_start(decay[:, :, :, :].rearrange("p b h s -> p (b h s)"),
                                 mscr.rearrange("h s -> (h s)").partition_broadcast(P)).then_inc(m_bc.sem, 16)
                if ok(p):
                    load(p)
                if isinstance(t, int) and t == -1:
                    for j in range(2, len(jobs)):
                        weights(j)
                if ok(u_):
                    sp.wait_ge(y_d.sem, y_d.at(u_, 2))
                    sp.dma_start(o_d[u_], xoo[:, 2:4, :]).then_inc(st_o.sem, 16)
            steps(sp, body)
            sp.wait_ge(st_o.sem, 16 * NP)

        @block.gpsimd
        def _(pool):
            def body(t):
                m, p = t + 1, t + 2
                if isinstance(t, int) and t == -2:
                    for tile, v in ((ident, 0.0), (tri, 1.0), (ntri, -1.0), (mhalf, -0.5)):
                        pool.memset(tile[:, :], v).then_inc(c_pool.sem, 1)
                    pool.memset(vaug[:, :, :, DH:DH + 1], 1.0).then_inc(c_pool.sem, 1)
                    for e in range(NE):
                        pool.memset(rev[:, :, e:e + 1], float(NE - e)).then_inc(c_pool.sem, 1)
                    pool.wait_ge(c_pool.sem, 5 + NE)
                    pool.affine_select(out=ident[:, :], in_=ident[:, :], compare_op=ALU.not_equal, fill=1.0, base=0,
                                       pattern=[[-1, P]], channel_multiplier=1).then_inc(c_pool.sem, 1)
                    for tile in (tri, ntri):
                        pool.affine_select(out=tile[:, :], in_=tile[:, :], compare_op=ALU.is_ge, fill=0.0, base=0,
                                           pattern=[[1, P]], channel_multiplier=-1).then_inc(c_pool.sem, 1)
                    pool.wait_ge(c_pool.sem, 8 + NE)
                    pool.tensor_copy(identh[:, :], ident[:, :]).then_inc(c_pool.sem, 1)
                if ok(m):
                    if past(m - 1):
                        pool.wait_ge(po_g.sem, po_g.at(m - 1, 3))
                    apart(pool, m - 1, passed)
                    pool.wait_ge(ld_x.sem, ld_x.at(m, 16))
                    apart(pool, m, passed)
                    pool.tensor_copy(xres[:, :, :], xin[:, :, :]).then_inc(cp_x.sem, 1)
                    if past(m - 1):
                        pool.wait_ge(qk_p.sem, qk_p.at(m - 1, 8))
                    apart(pool, m - 1, passed)
                    pool.wait_ge(ld_k.sem, ld_k.at(m, 16))
                    apart(pool, m, passed)
                    pool.tensor_copy(kT[:, :, :], kin[:, :, :]).then_inc(cp_k.sem, 1)
                    if past(m - 1):
                        pool.wait_ge(av_p.sem, av_p.at(m - 1, 4))
                    apart(pool, m - 1, passed)
                    pool.wait_ge(ld_v.sem, ld_v.at(m, 16))
                    apart(pool, m, passed)
                    pool.tensor_copy(vaug[:, :, :, 0:DH], vin[:, :, :].rearrange("p b (h e) -> p b h e", e=DH))\
                        .then_inc(cp_v.sem, 1)
                    pool.wait_ge(m_bc.sem, m_bc.at(m, 16))
                    apart(pool, m, passed)
                    pool.wait_ge(mx_d.sem, mx_d.at(m, 4))
                    apart(pool, m, passed)
                    for j in range(4):
                        a = acol[:, 8 * j:8 * j + 8].unsqueeze(2).to_broadcast([P, 8, P])
                        d = unit(j)
                        pool.tensor_tensor(d, a, d, ALU.subtract).then_inc(arg_g.sem, 1)
                    for j in range(4):
                        pool.wait_ge(dec_a.sem, dec_a.at(m, j + 1))
                        apart(pool, m, passed)
                        d = unit(j)
                        pool.affine_select(out=d, in_=d, compare_op=ALU.is_ge, fill=0.0, base=0,
                                           pattern=[[0, 8], [1, P]], channel_multiplier=-1)\
                            .then_inc(dec_g.sem, 1)
                if ok(p):
                    pool.wait_ge(ln1.sem, ln1.at(p, 3))
                    apart(pool, p, passed)
                    pool.tensor_scalar(rv[:, 0, 0, :], bn[:, 0, :, 7], EPS_LN, None, ALU.add).then_inc(rs1.sem, 1)
                    pool.wait_ge(rs1.sem, rs1.at(p, 1))
                    apart(pool, p, passed)
                    pool.tensor_tensor(rv[:, 0, 1, :], rv[:, 0, 0, :], mhalf[:, 0:2], ALU.pow).then_inc(rs1.sem, 1)
                if ok(m):
                    pool.wait_ge(po_d.sem, po_d.at(m, 6))
                    apart(pool, m, passed)
                    pool.tensor_tensor(st[:, 5, :], st[:, 4, :], mhalf[:, :], ALU.pow).then_inc(po_g.sem, 1)
                    pool.wait_ge(po_d.sem, po_d.at(m, 7))
                    apart(pool, m, passed)
                    if isinstance(t, int) and t == -1:
                        pool.wait_ge(c_dve.sem, 1)
                    pool.tensor_tensor(uc[:, :, :], uc[:, :, :], bc2(lnsg[:, :]), ALU.mult).then_inc(po_g.sem, 1)
                    pool.wait_ge(po_g.sem, po_g.at(m, 2))
                    apart(pool, m, passed)
                    if past(m - 1):
                        pool.wait_ge(xo_d.sem, xo_d.at(m - 1, 3))
                    apart(pool, m - 1, passed)
                    pool.tensor_tensor(x1[:, :, :], uc[:, :, :], xres[:, :, :], ALU.add).then_inc(po_g.sem, 1)
                    pool.wait_ge(ln2.sem, ln2.at(m, 3))
                    apart(pool, m, passed)
                    pool.tensor_scalar(rv[:, 1, 0, :], bn[:, 1, :, 7], EPS_LN, None, ALU.add).then_inc(rs2.sem, 1)
                    pool.wait_ge(rs2.sem, rs2.at(m, 1))
                    apart(pool, m, passed)
                    pool.tensor_tensor(rv[:, 1, 1, :], rv[:, 1, 0, :], mhalf[:, 0:2], ALU.pow).then_inc(rs2.sem, 1)
            steps(pool, body)

        @block.scalar
        def _(act):
            def gelu(n, i, second):
                done, src = (g1_a, del_p) if second else (g0_a, base_p)
                act.wait_ge(src.sem, src.at(n, i + 1))
                for k in range(2):
                    act.activation(hid[:, int(second), i % 2, k * T:(k + 1) * T], H[i % 2][:, k * T:(k + 1) * T],
                                   ACT.Gelu_apprx_tanh, bias=b1s[:, 2 * i + k:2 * i + k + 1], scale=1.0 / WS)\
                        .then_inc(done.sem, 1)

            def hi(n, i):
                act.wait_ge(v_d_.sem, v_d_.at(n, i + 1))
                prior = (n, i - 2) if i >= 2 else (n - 1, i - 2 + NS)
                if past(prior[0]):
                    act.wait_ge(w2_p.sem, w2_p.at(prior[0], prior[1] + 1))
                act.activation(gv[0][:, i % 2, 1, :], hid[:, 1, i % 2, :], ACT.Copy).then_inc(hi_a.sem, 1)
                act.wait_ge(g_d_.sem, g_d_.at(n, i + 1))
                act.activation(gv[0][:, i % 2, 0, :], hid[:, 0, i % 2, :], ACT.Copy).then_inc(hi_a.sem, 1)

            def weights(j):
                act.wait_ge(ld_w[j % 2].sem, 16 * sum(len(jobs[i][0]) for i in range(j % 2, j + 1, 2)))
                for c0, c1_, s, dst in jobs[j][1]:
                    act.activation(dst[0], stage[j % 2][:, c0:c1_], ACT.Copy, scale=s).then_inc(w_hi.sem, 1)

            def body(t):
                u_, m, p = t - 1, t + 1, t + 2
                first = isinstance(t, int) and t == -2
                if first:
                    act.wait_ge(ld_c.sem, 16 * NCONST)
                    act.activation(tg[:, 2:4], tg[:, 0:2], ACT.Tanh).then_inc(c_act.sem, 1)
                if isinstance(t, int) and t == -1:
                    for j in range(2):
                        weights(j)
                for i in range(NS):
                    if i == 0:
                        if ok(u_):
                            hi(u_, NS - 1)
                        if ok(t):
                            act.wait_ge(ro_d.sem, ro_d.at(t, 16))
                            act.activation(pe_[:, :], ex[:, :], ACT.Exp).then_inc(ro_e.sem, 1)
                            act.wait_ge(z_p.sem, z_p.at(t, 1))
                            rg = R[1]
                            if past(t - 1):
                                act.wait_ge(del_p.sem, del_p.at(t - 1, NS))
                            act.activation(zs[:, :, :].rearrange("p a b -> p (a b)"),
                                           rg[:, 0:T].bitcast(F16)[:, 0:2 * T], ACT.Copy).then_inc(z_s.sem, 1)
                            if past(t - 1):
                                act.wait_ge(v_d_.sem, v_d_.at(t - 1, NS))
                            act.activation(rb[:, :], rg[:, T:2 * T], ACT.Copy).then_inc(z_s.sem, 1)
                    elif ok(t):
                        hi(t, i - 1)
                    if ok(t):
                        gelu(t, i, False)
                    if i == 1 and ok(u_):
                        act.wait_ge(z2_p.sem, z2_p.at(u_, 1))
                        if past(u_ - 1):
                            act.wait_ge(y_p.sem, y_p.at(u_ - 1, 1))
                        act.activation(z2s[:, :, :].rearrange("p a b -> p (a b)"),
                                       U[:, 256:384].bitcast(F16)[:, 0:T], ACT.Copy).then_inc(z2_s.sem, 1)
                    if i == 3 and ok(m):
                        if past(m - 1):
                            act.wait_ge(em_p.sem, em_p.at(m - 1, 1))
                        act.wait_ge(mx_d.sem, mx_d.at(m, 4))
                        act.activation(em[:, :], FM[:, :], ACT.Exp, scale=-1.0).then_inc(em_a.sem, 1)
                        for j in range(4):
                            act.wait_ge(arg_g.sem, arg_g.at(m, j + 1))
                            d = unit(j)
                            act.activation(d, d, ACT.Exp).then_inc(dec_a.sem, 1)
                    if i == 4 and ok(m):
                        act.wait_ge(em_p.sem, em_p.at(m, 1))
                        if past(m - 1):
                            act.wait_ge(po_d.sem, po_d.at(m - 1, 2))
                        act.activation(emt[:, :], G[:, 480:512], ACT.Copy).then_inc(em_s.sem, 1)
                    if 4 <= i <= 6 and ok(m):
                        for g in {4: (0,), 5: (1, 2), 6: (3,)}[i]:
                            act.wait_ge(av_p.sem, av_p.at(m, g + 1))
                            if g == 0:
                                if past(m - 1):
                                    act.wait_ge(po_d.sem, po_d.at(m - 1, 4))
                            dst = u[:, (g // 2) * NH:(g // 2 + 1) * NH, :].rearrange("p (c q) e -> p q c e", q=4)
                            act.activation(dst[:, 2 * (g % 2):2 * (g % 2) + 2],
                                           G[:, 0:8 * (DH + 1)].rearrange("p (q c e) -> p q c e", q=2, c=4),
                                           ACT.Copy).then_inc(av_s.sem, 1)
                    if i == 6 and ok(p):
                        for b in range(2):
                            act.wait_ge(qt_p.sem, qt_p.at(p, b + 1))
                            act.activation(qT[:, :, b, :], R[b][:, :].rearrange("p (c s) -> p c s", c=DC), ACT.Copy)\
                                .then_inc(qt_s.sem, 1)
                    if i == 6 and ok(m):
                        act.wait_ge(po_d.sem, po_d.at(m, 2))
                        act.activation(st[:, 2, :], st[:, 1, :], ACT.Square, bias=EPS ** 1.5, scale=EPS ** 0.5)\
                            .then_inc(po_a.sem, 1)
                        act.wait_ge(po_d.sem, po_d.at(m, 4))
                        if ok(p):
                            act.wait_ge(qt_p.sem, qt_p.at(p, 2))
                        act.activation(qn[:, :, :], uc[:, :, :], ACT.Square).then_inc(po_a.sem, 1)
                    if ok(t):
                        gelu(t, i, True)
                    elif isinstance(t, int) and t == -1:
                        weights(i + 2)
                if ok(p):
                    act.wait_ge(gat_s.sem, gat_s.at(p, 2))
                    act.activation(gt[:, 1, :], gt[:, 0, :], ACT.Exp).then_inc(gat_e.sem, 1)
                    act.wait_ge(gat_e.sem, gat_e.at(p, 1))
                    act.activation(gt[:, 2, :], gt[:, 1, :], ACT.Ln, bias=1.0).then_inc(gat_e.sem, 1)
                if ok(m):
                    for b in range(2):
                        act.wait_ge(xt_p.sem, xt_p.at(m, b + 1))
                        if past(m - 1):
                            act.wait_ge(base_p.sem, base_p.at(m - 1, NS))
                        act.activation(xT[0][:, :, b * P:(b + 1) * P],
                                       R[b][:, :].rearrange("p (c s) -> p c s", c=DC), ACT.Copy).then_inc(xt_h.sem, 1)
            steps(act, body)

        @block.vector
        def _(dve):
            tt, ts, stt = dve.tensor_tensor, dve.tensor_scalar, dve.scalar_tensor_tensor

            def combine(n, i):
                h0, h1 = hid[:, 0, i % 2, :], hid[:, 1, i % 2, :]
                dve.wait_ge(g1_a.sem, g1_a.at(n, 2 * i + 2))
                if i == 0:
                    dve.wait_ge(z_s.sem, z_s.at(n, 2))
                pair = "p (k t) -> p k t"
                tt(h1.rearrange(pair, k=2), h1.rearrange(pair, k=2), bc2(rb[:, :]), ALU.mult).then_inc(v_d_.sem, 1)
                dve.wait_ge(v_d_.sem, v_d_.at(n, i + 1))
                tt(h0, h0, h1, ALU.add).then_inc(g_d_.sem, 1)
                dve.wait_ge(hi_a.sem, hi_a.at(n, 2 * i + 1))
                tt(gv[1][:, i % 2, 1, :], h1, gv[0][:, i % 2, 1, :], ALU.subtract).then_inc(lo_d.sem, 1)
                dve.wait_ge(g_d_.sem, g_d_.at(n, i + 1))
                dve.wait_ge(hi_a.sem, hi_a.at(n, 2 * i + 2))
                tt(gv[1][:, i % 2, 0, :], h0, gv[0][:, i % 2, 0, :], ALU.subtract).then_inc(lo_d.sem, 1)

            def norm_stats(src, which, n, count, ready):
                for b in range(2):
                    dve.bn_stats(bn[:, which, b, 0:6], src[:, b, :])
                raise AssertionError

            def router(n):
                first, second = rt[:, 2:2 + 2 * NE], rt[:, 2 + 2 * NE:2 + 4 * NE]
                oh0 = first.rearrange("p (b e) -> p b e", b=2)
                oh1 = second.rearrange("p (b e) -> p b e", b=2)
                k = [0]

                def step(ins, fence=True):
                    ins.then_inc(ro_d.sem, 1)
                    k[0] += 1
                    if fence:
                        dve.wait_ge(ro_d.sem, ro_d.at(n, k[0]))

                def be(i):
                    return mx[:, i, :].unsqueeze(2).to_broadcast([P, 2, NE])

                ps = R[0][:, 0:2 * AC].rearrange("p (b k) -> p b k", b=2)
                dve.wait_ge(ro_p.sem, ro_p.at(n, 1))
                step(ts(u1s[:, :, :].rearrange("p (b e) r -> p b (e r)", b=2), ps[:, :, 0:R64], 1.0 / WS, None, ALU.mult), False)
                step(stt(lg[:, :, :], ps[:, :, R64:AC], 1.0 / WS, brb[:, :, :], ALU.mult, ALU.add))
                step(dve.tensor_reduce(mx[:, 0, :], lg[:, :, :], AX, ALU.max))
                step(tt(eq[:, :, :], lg[:, :, :], be(0), ALU.is_equal))
                step(tt(eq[:, :, :], eq[:, :, :], rev[:, :, :], ALU.mult))
                step(dve.tensor_reduce(mx[:, 1, :], eq[:, :, :], AX, ALU.max))
                step(tt(oh0, eq[:, :, :], be(1), ALU.is_equal))
                step(stt(l2[:, :, :], oh0, -1e30, lg[:, :, :], ALU.mult, ALU.add))
                step(dve.tensor_reduce(mx[:, 2, :], l2[:, :, :], AX, ALU.max))
                step(tt(eq[:, :, :], l2[:, :, :], be(2), ALU.is_equal), False)
                step(tt(ex[:, 0:2 * NE].rearrange("p (b e) -> p b e", b=2), lg[:, :, :], be(0), ALU.subtract), False)
                step(tt(ex[:, 2 * NE:2 * NE + 2], mx[:, 2, :], mx[:, 0, :], ALU.subtract))
                step(tt(eq[:, :, :], eq[:, :, :], rev[:, :, :], ALU.mult))
                step(dve.tensor_reduce(mx[:, 3, :], eq[:, :, :], AX, ALU.max))
                step(tt(oh1, eq[:, :, :], be(3), ALU.is_equal))
                step(tt(ohd[:, :, :], oh1, oh0, ALU.subtract))
                for i, oh in enumerate((first, ohd[:, :, :].rearrange("p b e -> p (b e)"))):
                    step(tt(zf[:, i], u1s[:, :, :], oh.unsqueeze(2).to_broadcast([P, 2 * NE, RK]), ALU.mult), i == 1)
                zfv = zf[:, :, :, :].rearrange("p i (b e) r -> p (i b) (e r)", b=2)
                step(dve.tensor_copy(zsp[:, :, 0, :], zfv))
                step(tt(zsp[:, :, 1, :], zfv, zsp[:, :, 0, :], ALU.subtract))
                dve.wait_ge(ro_e.sem, ro_e.at(n, 1))
                step(dve.tensor_reduce(mx[:, 4, :], pe_[:, 0:2 * NE].rearrange("p (b e) -> p b e", b=2), AX, ALU.add))
                step(dve.reciprocal(mx[:, 5, :], mx[:, 4, :]))
                step(ts(rt[:, 0:2], mx[:, 5, :], tg[:, 1:2], None, ALU.mult), False)
                step(stt(c2[:, :], pe_[:, 2 * NE:2 * NE + 2], 1.0, mx[:, 5, :], ALU.add, ALU.mult), False)
                step(dve.tensor_copy(mx[:, 1, :], mx[:, 5, :]))
                assert k[0] == ro_d.per

            def weights(j):
                done = sum(parts[:j])
                for i, (c0, c1_, s, dst) in enumerate(jobs[j][1]):
                    dve.wait_ge(w_hi.sem, done + i + 1)
                    stt(dst[1], stage[j % 2][:, c0:c1_], s, dst[0], ALU.mult, ALU.subtract).then_inc(w_lo.sem, 1)

            def body(t):
                u_, m, p = t - 1, t + 1, t + 2
                if isinstance(t, int) and t == -2:
                    dve.wait_ge(c_act.sem, 1)
                    ts(lnsg[:, :], lnsg[:, :], tg[:, 2:3], None, ALU.mult).then_inc(c_dve.sem, 1)
                    ts(b2g[:, :], b2g[:, :], tg[:, 3:4], None, ALU.mult).then_inc(c_dve.sem, 1)
                    ts(tg[:, 1:2], tg[:, 3:4], 1.0 / WS, None, ALU.mult).then_inc(c_dve.sem, 1)
                    tt(wg[:, DC:2 * DC, :], wg[:, DC:2 * DC, :], wg[:, 2 * DC:3 * DC, :], ALU.add).then_inc(c_dve.sem, 1)
                    dve.wait_ge(c_dve.sem, 4)
                if isinstance(t, int) and t == -1:
                    for j in range(2):
                        weights(j)
                for i in range(NS):
                    if i == 0:
                        if ok(u_):
                            combine(u_, NS - 1)
                        if ok(t):
                            if isinstance(t, int) and t == 0:
                                dve.wait_ge(c_pool.sem, 9 + NE)
                            router(t)
                        if ok(m):
                            dve.wait_ge(lf_p.sem, lf_p.at(m, 1))
                            dve.tensor_copy(aT[:, :], G[0:HB, 64:192]).then_inc(mx_d.sem, 1)
                            dve.wait_ge(mx_d.sem, mx_d.at(m, 1))
                            if past(m - 1):
                                dve.wait_ge(m_wr.sem, m_wr.at(m - 1, 16))
                            dve.tensor_tensor_scan(MT[:, :], aT[:, :], aT[:, :], -3.0e38, ALU.max, ALU.max)\
                                .then_inc(mx_d.sem, 1)
                            dve.wait_ge(mx_d.sem, mx_d.at(m, 2))
                            if past(m - 1):
                                dve.wait_ge(em_a.sem, em_a.at(m - 1, 1))
                            tt(FM[:, :], G[0:HB, 192:320], MT[:, :], ALU.add).then_inc(mx_d.sem, 1)
                            if past(m - 1):
                                dve.wait_ge(arg_g.sem, arg_g.at(m - 1, 4))
                            tt(acol[:, :], G[:, 320:352], gb[:, 0:HB], ALU.add).then_inc(mx_d.sem, 1)
                    elif ok(t):
                        combine(t, i - 1)
                    if i == 1 and ok(u_):
                        dve.wait_ge(w2_p.sem, w2_p.at(u_, NS))
                        uu = U[:, 0:256].rearrange("p (b k) -> p b k", b=2)
                        flat = "p (b e) r -> p b (e r)"
                        bce = [rtk[:, 2 + 2 * NE * c:2 + 2 * NE * (c + 1)].unsqueeze(2).to_broadcast([P, 2 * NE, RK])
                               for c in range(2)]
                        ts(uv[:, 0].rearrange(flat, b=2), uu[:, :, R64:2 * R64], 1.0 / WS, None, ALU.mult)\
                            .then_inc(z2_d.sem, 1)
                        dve.wait_ge(z2_d.sem, z2_d.at(u_, 1))
                        stt(uv[:, 1].rearrange(flat, b=2), uu[:, :, 0:R64], 1.0 / WS, uv[:, 0].rearrange(flat, b=2),
                            ALU.mult, ALU.subtract).then_inc(z2_d.sem, 1)
                        tt(uv[:, 2], uv[:, 0], bce[1], ALU.mult).then_inc(z2_d.sem, 1)
                        dve.wait_ge(z2_d.sem, z2_d.at(u_, 3))
                        tt(uv[:, 3], uv[:, 1], bce[0], ALU.mult).then_inc(z2_d.sem, 1)
                        dve.wait_ge(z2_d.sem, z2_d.at(u_, 4))
                        tt(uv[:, 0], uv[:, 2], uv[:, 3], ALU.add).then_inc(z2_d.sem, 1)
                        dve.wait_ge(z2_d.sem, z2_d.at(u_, 5))
                        dve.tensor_copy(z2sp[:, :, 0, :], uv[:, 0].rearrange(flat, b=2)).then_inc(z2_d.sem, 1)
                        dve.wait_ge(z2_d.sem, z2_d.at(u_, 6))
                        tt(z2sp[:, :, 1, :], uv[:, 0].rearrange(flat, b=2), z2sp[:, :, 0, :], ALU.subtract)\
                            .then_inc(z2_d.sem, 1)
                        dve.wait_ge(y_p.sem, y_p.at(u_, 1))
                        if past(u_ - 1):
                            dve.wait_ge(st_o.sem, st_o.at(u_ - 1, 16))
                        for b in range(2):
                            stt(xoo[:, 2 + b, :], Y[b][:, :], rtk[:, b:b + 1], xoo[:, b, :], ALU.mult, ALU.add)\
                                .then_inc(y_d.sem, 1)
                    if i == 3 and ok(t):
                        if past(t - 1):
                            dve.wait_ge(y_d.sem, y_d.at(t - 1, 2))
                        dve.tensor_copy(rtk[:, :], rt[:, :]).then_inc(xo_d.sem, 1)
                        for b in range(2):
                            stt(xoo[:, b, :], b2g[:, :], c2[:, b:b + 1], x1[:, b, :], ALU.mult, ALU.add)\
                                .then_inc(xo_d.sem, 1)
                    if 4 <= i <= 5 and ok(m):
                        for r in range(4 * (i - 4), 4 * (i - 3)):
                            dve.wait_ge(qk_p.sem, qk_p.at(m, r + 1))
                            dve.wait_ge(dec_g.sem, dec_g.at(m, 2 * (r // 4) + 2))
                            if r >= 3:
                                dve.wait_ge(av_p.sem, av_p.at(m, (r - 3) // 2 + 1))
                            else:
                                if past(m - 1):
                                    dve.wait_ge(av_p.sem, av_p.at(m - 1, 4))
                            d = decay[:, r // 4].rearrange("p (c q) s -> p q c s", q=4)[:, r % 4]
                            stt(Ct[:, r % 3], R[r % 2][:, :].rearrange("p (c s) -> p c s", c=4), SC, d,
                                ALU.mult, ALU.mult).then_inc(c_d.sem, 1)
                    if i == 5 and ok(p):
                        dve.wait_ge(ld_x.sem, ld_x.at(p, 16))
                        for b in range(2):
                            dve.bn_stats(bn[:, 0, b, 0:6], xin[:, b, :]).then_inc(ln1.sem, 1)
                        dve.wait_ge(ln1.sem, ln1.at(p, 2))
                        if past(p - 1):
                            dve.wait_ge(rs1.sem, rs1.at(p - 1, 2))
                        apart(dve, p - 1, passed)
                        dve.bn_aggr(bn[:, 0, 0, 6:8], bn[:, 0, 0, 0:6])
                        dve.bn_aggr(bn[:, 0, 1, 6:8], bn[:, 0, 1, 0:6]).then_inc(ln1.sem, 1)
                        dve.wait_ge(rs1.sem, rs1.at(p, 2))
                        for b in range(2):
                            ts(qn[:, b, :], xin[:, b, :], bn[:, 0, b, 6:7], rv[:, 0, 1, b:b + 1], ALU.subtract, ALU.mult)\
                                .then_inc(q_nd.sem, 1)
                    if i == 6 and ok(m):
                        dve.wait_ge(av_s.sem, av_s.at(m, 4))
                        dve.wait_ge(em_s.sem, em_s.at(m, 1))
                        stt(st[:, 0, :], u[:, :, DH], -1.0, u[:, :, DH], ALU.mult, ALU.max).then_inc(po_d.sem, 1)
                        dve.wait_ge(po_d.sem, po_d.at(m, 1))
                        tt(st[:, 1, :], st[:, 0, :], emt[:, :], ALU.max).then_inc(po_d.sem, 1)
                        dve.tensor_reduce(st[:, 3, :], u[:, :, 0:DH], AX, ALU.add).then_inc(po_d.sem, 1)
                        dve.wait_ge(po_d.sem, po_d.at(m, 3))
                        if past(m - 1):
                            dve.wait_ge(xt_p.sem, xt_p.at(m - 1, 2))
                        ucv = uc[:, :, :].rearrange("p b (h e) -> p (b h) e", e=DH)
                        stt(ucv, st[:, 3, :].unsqueeze(2).to_broadcast([P, HB, DH]), -1.0 / DH, u[:, :, 0:DH],
                            ALU.mult, ALU.add).then_inc(po_d.sem, 1)
                        dve.wait_ge(po_a.sem, po_a.at(m, 2))
                        dve.tensor_reduce(st[:, 6, :], qn[:, :, :].rearrange("p b (h e) -> p (b h) e", e=DH), AX, ALU.add)\
                            .then_inc(po_d.sem, 1)
                        dve.wait_ge(po_d.sem, po_d.at(m, 5))
                        stt(st[:, 4, :], st[:, 6, :], 1.0 / DH, st[:, 2, :], ALU.mult, ALU.add).then_inc(po_d.sem, 1)
                        dve.wait_ge(po_g.sem, po_g.at(m, 1))
                        tt(ucv, ucv, st[:, 5, :].unsqueeze(2).to_broadcast([P, HB, DH]), ALU.mult).then_inc(po_d.sem, 1)
                    if i == 6 and ok(p):
                        dve.wait_ge(gat_p.sem, gat_p.at(p, 1))
                        tt(gb[:, :], G[:, 0:4 * NH], bg[:, :], ALU.add).then_inc(gat_s.sem, 1)
                        dve.wait_ge(gat_s.sem, gat_s.at(p, 1))
                        stt(gt[:, 0, :], gb[:, HB:], -1.0, gb[:, HB:], ALU.mult, ALU.min).then_inc(gat_s.sem, 1)
                    if isinstance(t, int) and t == -1:
                        weights(i + 2)
                if ok(m):
                    dve.wait_ge(po_g.sem, po_g.at(m, 3))
                    for b in range(2):
                        dve.bn_stats(bn[:, 1, b, 0:6], x1[:, b, :]).then_inc(ln2.sem, 1)
                    dve.wait_ge(ln2.sem, ln2.at(m, 2))
                    apart(dve, m, passed)
                    dve.bn_aggr(bn[:, 1, 0, 6:8], bn[:, 1, 0, 0:6])
                    dve.bn_aggr(bn[:, 1, 1, 6:8], bn[:, 1, 1, 0:6]).then_inc(ln2.sem, 1)
                if ok(p):
                    dve.wait_ge(gat_e.sem, gat_e.at(p, 2))
                    stt(gt[:, 3, :], gb[:, HB:], 0.0, gt[:, 2, :], ALU.min, ALU.subtract).then_inc(lf_d.sem, 1)
                if ok(m):
                    dve.wait_ge(rs2.sem, rs2.at(m, 2))
                    for b in range(2):
                        ts(uc[:, b, :], x1[:, b, :], bn[:, 1, b, 6:7], rv[:, 1, 1, b:b + 1], ALU.subtract, ALU.mult)\
                            .then_inc(xn_d.sem, 1)
                    for b in range(2):
                        dve.wait_ge(xt_h.sem, xt_h.at(m, b + 1))
                        sl = slice(b * P, (b + 1) * P)
                        tt(xT[1][:, :, sl], R[b][:, :].rearrange("p (c s) -> p c s", c=DC), xT[0][:, :, sl],
                           ALU.subtract).then_inc(xt_l.sem, 1)
            steps(dve, body)

        @block.tensor
        def _(pe):
            def mm(out_, l, r, start, stop=False):
                return pe.matmul(out_, l, r, start=start, stop=stop, skip_group_check=True)

            def base(n, i):
                prior = (n, i - 2) if i >= 2 else (n - 1, i - 2 + NS)
                if past(prior[0]):
                    pe.wait_ge(g1_a.sem, g1_a.at(prior[0], 2 * prior[1] + 2))
                for k in range(2):
                    f = 2 * i + k
                    for c in range(DC):
                        for a, b in ((0, 0), (0, 1), (1, 0)):
                            mm(H[i % 2][:, k * T:(k + 1) * T], w1[a][:, c, f * P:(f + 1) * P], xT[b][:, c, :],
                               start=(k == 0 and c == 0 and a == 0 and b == 0))

            def lora(n, i, which, done):
                for k in range(2):
                    f = 2 * i + k
                    for a in range(2):
                        last = mm(H[i % 2][:, k * T:(k + 1) * T], b1w[a][:, f * P:(f + 1) * P], zs[:, which, :],
                                  start=False, stop=(a == 1))
                last.then_inc(done.sem, 1)

            def delta(n, i):
                pe.wait_ge(g0_a.sem, g0_a.at(n, 2 * i + 2))
                lora(n, i, 1, del_p)

            def second(n, i):
                pe.wait_ge(lo_d.sem, lo_d.at(n, 2 * i + 1))
                for what in (1, 0):
                    if what == 0:
                        pe.wait_ge(lo_d.sem, lo_d.at(n, 2 * i + 2))
                    for k in range(2):
                        f = 2 * i + k
                        for b in range(2):
                            tok = slice(k * T + b * P, k * T + (b + 1) * P)
                            uo = U[:, b * P + what * R64:b * P + (what + 1) * R64]
                            for a, w in ((0, 0), (0, 1), (1, 0)):
                                l = gv[a][:, i % 2, what, tok]
                                last = mm(uo, l, a2[w][:, f, :],
                                          start=(what == 1 and i == 0 and k == 0 and b == 0 and a == 0 and w == 0))
                                if what == 0:
                                    last = mm(Y[b][:, :], l, w2[w][:, f, :],
                                              start=(i == 0 and k == 0 and a == 0 and w == 0))
                last.then_inc(w2_p.sem, 1)

            def body(t):
                u_, m, p = t - 1, t + 1, t + 2
                if isinstance(t, int) and t == -2:
                    pe.wait_ge(c_pool.sem, 9 + NE)
                    pe.wait_ge(c_dve.sem, 4)
                if isinstance(t, int) and t == 0:
                    pe.wait_ge(w_hi.sem, sum(parts))
                    pe.wait_ge(w_lo.sem, sum(parts))
                for i in range(NS):
                    if ok(t):
                        if i == 0:
                            pe.wait_ge(xt_l.sem, xt_l.at(t, 2))
                            for b in range(2):
                                for c in range(DC):
                                    for a, w in ((0, 0), (0, 1), (1, 0)):
                                        last = mm(R[0][:, b * AC:(b + 1) * AC], xT[a][:, c, b * P:(b + 1) * P],
                                                  a1[w][:, c, :], start=(c == 0 and a == 0 and w == 0),
                                                  stop=(c == DC - 1 and a == 1))
                            last.then_inc(ro_p.sem, 1)
                        base(t, i)
                        if i == 0:
                            pe.wait_ge(ro_d.sem, ro_d.at(t, 20))
                            for j in range(4):
                                pe.transpose(R[1][:, j * R64:(j + 1) * R64].bitcast(F16)[:, 0:P],
                                             zsp[:, j].rearrange("p a r -> p (a r)"), identh[:, :])
                            pe.wait_ge(ro_e.sem, ro_e.at(t, 1))
                            for b in range(2):
                                last = pe.transpose(R[1][:, T + b * P:T + (b + 1) * P],
                                                    pe_[:, 2 * NE + b:2 * NE + b + 1].to_broadcast([P, P]), ident[:, :])
                            last.then_inc(z_p.sem, 1)
                            pe.wait_ge(z_s.sem, z_s.at(t, 1))
                        lora(t, i, 0, base_p)
                    if i == 1 and ok(u_):
                        pe.wait_ge(z2_d.sem, z2_d.at(u_, 7))
                        for b in range(2):
                            last = pe.transpose(U[:, 256 + b * R64:256 + (b + 1) * R64].bitcast(F16)[:, 0:P],
                                                z2sp[:, b].rearrange("p a r -> p (a r)"), identh[:, :])
                        last.then_inc(z2_p.sem, 1)
                    if i in (4, 5) and ok(m):
                        if i == 4:
                            pe.wait_ge(cp_k.sem, cp_k.at(m, 1))
                            apart(pe, m, passed)
                            pe.wait_ge(em_a.sem, em_a.at(m, 1))
                            apart(pe, m, passed)
                            pe.transpose(G[:, 480:512], em[:, :], ident[0:HB, 0:HB]).then_inc(em_p.sem, 1)
                        scores(m, 4 * (i - 4), t)
                        if i == 5:
                            products(m, 1)
                    if i == 6 and ok(m):
                        products(m, 3)
                    if i == 6 and ok(p):
                        for b in range(2):
                            pe.wait_ge(q_nd.sem, q_nd.at(p, b + 1))
                            if ok(m):
                                pe.wait_ge(c_d.sem, c_d.at(m, 7 + b))
                            for c in range(DC):
                                last = pe.transpose(R[b][:, c * P:(c + 1) * P], qn[:, b, c * P:(c + 1) * P], ident[:, :])
                            last.then_inc(qt_p.sem, 1)
                    if i == 0:
                        if ok(u_):
                            second(u_, NS - 1)
                        if ok(t):
                            delta(t, 0)
                    elif i == 1:
                        if ok(u_):
                            pe.wait_ge(z2_s.sem, z2_s.at(u_, 1))
                            for b in range(2):
                                for a in range(2):
                                    last = mm(Y[b][:, :], z2s[:, b, :], b2w[a][:, :], start=False, stop=(a == 1))
                            last.then_inc(y_p.sem, 1)
                        if ok(t):
                            delta(t, 1)
                            if past(t - 1):
                                pe.wait_ge(y_d.sem, y_d.at(t - 1, 2))
                            second(t, 0)
                    elif ok(t):
                        second(t, i - 1)
                        delta(t, i)
                    if i == 4 and ok(m):
                        scores(m, 2, t)
                        products(m, 0)
                    if i == 5 and ok(m):
                        scores(m, 6, t)
                        products(m, 2)
                    if i == 6 and ok(p):
                        if ok(m):
                            pe.wait_ge(av_s.sem, av_s.at(m, 4))
                        pe.wait_ge(ld_k.sem, ld_k.at(p, 16))
                        pe.wait_ge(qt_s.sem, qt_s.at(p, 2))
                        for b in range(2):
                            o = G[:, 0:4 * NH].rearrange("p (k b h) -> p k b h", k=2, b=2)[:, :, b, :]
                            for c in range(2 * DC):
                                l = qT[:, c, b, :] if c < DC else kin[:, c - DC, b * P:(b + 1) * P]
                                last = mm(o, l, wg[:, c, :].rearrange("p (k h) -> p k h", k=2), start=(c == 0),
                                          stop=(c == 2 * DC - 1))
                        last.then_inc(gat_p.sem, 1)
                if ok(p):
                    pe.wait_ge(lf_d.sem, lf_d.at(p, 1))
                    lf = gt[:, 3, :]
                    mm(G[:, 320:352], ntri[:, :], lf, True, True)
                    mm(G[0:HB, 64:192], gb[:, 0:HB], ident[:, :], True)
                    mm(G[0:HB, 64:192], lf, ntri[:, :], False, True)
                    mm(G[0:HB, 192:320], lf, tri[:, :], True, True).then_inc(lf_p.sem, 1)
                if ok(m):
                    for b in range(2):
                        pe.wait_ge(xn_d.sem, xn_d.at(m, b + 1))
                        if ok(p):
                            pe.wait_ge(qt_s.sem, qt_s.at(p, b + 1))
                        for c in range(DC):
                            last = pe.transpose(R[b][:, c * P:(c + 1) * P], uc[:, b, c * P:(c + 1) * P], ident[:, :])
                        last.then_inc(xt_p.sem, 1)

            def scores(m, r0, t):
                for r in (r0, r0 + 1):
                    if r >= 2:
                        pe.wait_ge(c_d.sem, c_d.at(m, r - 1))
                    elif ok(t):
                        pe.wait_ge(ro_d.sem, ro_d.at(t, 2))
                        pe.wait_ge(z_s.sem, z_s.at(t, 2))
                    q, b = r % 4, r // 4
                    rows = slice(DH * q, DH * (q + 1))
                    for c in range(DC):
                        last = mm(R[r % 2][:, c * P:(c + 1) * P], kT[rows, c, b * P:(b + 1) * P], qT[rows, c, b, :],
                                  start=True, stop=True)
                    last.then_inc(qk_p.sem, 1)

            def products(m, g):
                if g == 0:
                    pe.wait_ge(em_s.sem, em_s.at(m, 1))
                    pe.wait_ge(cp_v.sem, cp_v.at(m, 1))
                else:
                    pe.wait_ge(av_s.sem, av_s.at(m, g))
                for r in (2 * g, 2 * g + 1):
                    pe.wait_ge(c_d.sem, c_d.at(m, r + 1))
                    for c in range(4):
                        o = ((r % 2) * 4 + c) * (DH + 1)
                        last = mm(G[:, o:o + DH + 1], Ct[:, r % 3, c, :], vaug[:, r // 4, 4 * c + r % 4, :],
                                  start=True, stop=True)
                last.then_inc(av_p.sem, 1)
            steps(pe, body)


def kernel(x, ctx_2048, g_xattn, g_ffn, L0_xattn_Wi, L0_xattn_bi, L0_xattn_Wf, L0_xattn_bf, L0_xattn_ln_scale,
           L0_ffn_W_r, L0_ffn_b_r, L0_ffn_W1, L0_ffn_b1, L0_ffn_W2, L0_ffn_b2, L0_ffn_A1, L0_ffn_B1, L0_ffn_A2,
           L0_ffn_B2):
    import numpy as np
    import concourse.bacc as bacc
    from concourse import mybir as mb
    from concourse.bass_utils import run_bass_kernel_spmd as run

    A = np.asarray
    nb, s, d = A(x).shape
    e, f, r = A(L0_ffn_B1).shape
    ctx = A(ctx_2048)
    wgate = np.concatenate([A(L0_xattn_Wi), A(L0_xattn_Wf)], axis=1)
    arrays = {
        "x": A(x),
        "ctx_tok": ctx,
        "ctx_T": ctx.reshape(nb // 2, 2 * s, d).transpose(0, 2, 1),
        "gx": A(g_xattn), "gf": A(g_ffn),
        "wgate": wgate.reshape(-1, 128, wgate.shape[1]).transpose(1, 0, 2),
        "bgate": np.concatenate([A(L0_xattn_bi)] * 2 + [A(L0_xattn_bf)] * 2),
        "lnscale": A(L0_xattn_ln_scale),
        "w1t": A(L0_ffn_W1).T, "w2t": A(L0_ffn_W2).T,
        "b1c": A(L0_ffn_b1).reshape(-1, 128).T, "b2": A(L0_ffn_b2),
        "a1r": np.concatenate([A(L0_ffn_A1).reshape(e * r, d).T, A(L0_ffn_W_r).T], axis=1),
        "br": A(L0_ffn_b_r),
        "b1lo": A(L0_ffn_B1).transpose(0, 2, 1).reshape(e * r, f),
        "a2t": A(L0_ffn_A2).reshape(e * r, f).T,
        "b2lo": A(L0_ffn_B2).transpose(0, 2, 1).reshape(e * r, d),
    }
    nc = bacc.Bacc("TRN2", target_bir_lowering=False, num_devices=1)
    ins, args = {}, []
    for name, a in arrays.items():
        a = np.ascontiguousarray(a)
        ins["in_" + name] = a
        args.append(nc.dram_tensor("in_" + name, a.shape, mb.dt.from_np(a.dtype), kind="ExternalInput").ap())
    args.append(nc.dram_tensor("out_0", A(x).shape, mb.dt.float32, kind="ExternalOutput").ap())
    flamingo_kernel(nc, *args)
    res = run(nc, [ins], core_ids=[0])
    return res.results[0]["out_0"]
```

```python
from contextlib import ExitStack

import concourse.bass as bass
from concourse import mybir

F32 = mybir.dt.float32
F16 = mybir.dt.float16
ALU = mybir.AluOpType
ACT = mybir.ActivationFunctionType
AX = mybir.AxisListType.X

P = 128
WS = 64.0
LORA = 2.0
EPS_LN = 1e-5
EPS = 1e-6


class Count:

    def __init__(self, sem, per):
        self.sem, self.per = sem, per

    def at(self, n, k):
        return n * self.per + k


def past(n):
    return not isinstance(n, int) or n >= 0


def apart(eng, n, passed):
    if not isinstance(n, int):
        eng.sem_inc(passed.sem)


def flamingo_kernel(nc, x, ctx_tok, ctx_T, gx, gf, wgate, bgate, lnscale, w1t, w2t, b1c, b2, a1r, br, b1lo, a2t, b2lo,
                    out):
    NB, S, D = x.shape
    NP = NB // 2
    DC = D // P
    NH = wgate.shape[2] // 2
    DH = D // NH
    FF = w1t.shape[1]
    FC = FF // P
    NS = FC // 2
    NE = br.shape[0]
    R64 = b1lo.shape[0]
    RK = R64 // NE
    T = 2 * S
    HB = 2 * NH
    NR = 8
    SC = float(DH) ** -0.5
    AC = R64 + NE
    assert S == P and NS == 8 and NH == 16 and DH == 32 and T * 2 == 512

    x_d = x.rearrange("(n b) s d -> n s b d", b=2)
    v_d = ctx_tok.rearrange("(n b) s d -> n s b d", b=2)
    k_d = ctx_T.rearrange("n (c p) t -> n p c t", p=P)
    o_d = out.rearrange("(n b) s d -> n s b d", b=2)

    with ExitStack() as ctx:
        def sb(name, shape, dt=F32):
            return ctx.enter_context(nc.sbuf_tensor(name, shape, dt))

        def cnt(name, per):
            return Count(ctx.enter_context(nc.semaphore(name)), per)

        Y = [ctx.enter_context(nc.psum_tensor(f"y{b}", [P, D], F32)) for b in range(2)]
        U = ctx.enter_context(nc.psum_tensor("u_lora", [P, 512], F32))
        H = [ctx.enter_context(nc.psum_tensor(f"hid{b}", [P, 512], F32)) for b in range(2)]
        R = [ctx.enter_context(nc.psum_tensor(f"ring{b}", [P, 512], F32)) for b in range(2)]
        G = ctx.enter_context(nc.psum_tensor("gates_av", [P, 512], F32))

        w1 = [sb(f"w1_{i}", [P, DC, FF], F16) for i in "hl"]
        w2 = [sb(f"w2_{i}", [P, FC, D], F16) for i in "hl"]
        b1w = [sb(f"b1w_{i}", [P, FF], F16) for i in "hl"]
        a2 = [sb(f"a2_{i}", [P, FC, R64], F16) for i in "hl"]
        a1 = [sb(f"a1_{i}", [P, DC, AC], F16) for i in "hl"]
        b2w = [sb(f"b2w_{i}", [P, D], F16) for i in "hl"]
        wg = sb("wg", [P, 3 * DC, 2 * NH])
        b1s = sb("b1s", [P, FC])
        bg = sb("bg", [P, 4 * NH])
        lnsg = sb("lnsg", [P, D])
        b2g = sb("b2g", [P, D])
        brb = sb("brb", [P, 2, NE])
        tg = sb("tg", [P, 4])
        ident = sb("ident", [P, P])
        identh = sb("identh", [P, P], F16)
        tri = sb("tri", [P, P])
        ntri = sb("ntri", [P, P])
        rev = sb("rev", [P, 2, NE])
        mhalf = sb("mhalf", [P, HB])
        euler = sb("euler", [P, 2 * NE + 2])
        xin = sb("xin", [P, 2, D])
        xres = sb("xres", [P, 2, D])
        kin = sb("kin", [P, DC, T])
        kT = sb("kT", [P, DC, T])
        vin = sb("vin", [P, 2, D])
        vaug = [sb(f"vaug_{i}", [P, 2, NH, DH + 1], F16) for i in "hl"]
        qn = sb("qn", [P, 2, D])
        qT = sb("qT", [P, DC, 2, P])
        gb = sb("gb", [P, 4 * NH])
        gt = sb("gt", [P, 4, HB])
        aT = sb("aT", [HB, P])
        MT = sb("MT", [HB, P])
        FM = sb("FM", [HB, P])
        em = sb("em", [HB, P])
        emt = sb("emt", [P, HB])
        acol = sb("acol", [P, HB])
        decay = sb("decay", [P, 2, NH, P])
        Ct = sb("Ct", [P, 2, 4, P])
        Cs = [sb(f"C_{i}", [P, 4, 4, P], F16) for i in "hl"]
        u = sb("u", [P, HB, DH + 1])
        uc = sb("uc", [P, 2, D])
        st = sb("st", [P, 8, HB])
        bn = sb("bn", [P, 2, 2, 8])
        rv = sb("rv", [P, 2, 2, 2])
        x1 = sb("x1", [P, 2, D])
        xT = [sb(f"xT_{i}", [P, DC, T], F16) for i in "hl"]
        lg = sb("lg", [P, 2, NE])
        l2 = sb("l2", [P, 2, NE])
        eq = sb("eq", [P, 2, NE])
        mx = sb("mx", [P, 6, 2])
        ex = sb("ex", [P, 2 * NE + 2])
        pe_ = sb("pe_", [P, 2 * NE + 2])
        rt = sb("rt", [P, 2 + 4 * NE])
        rtk = sb("rtk", [P, 2 + 4 * NE])
        ohd = sb("ohd", [P, 2, NE])
        c2 = sb("c2", [P, 2])
        u1s = sb("u1s", [P, 2 * NE, RK])
        zf = sb("zf", [P, 2, 2 * NE, RK])
        zsp = sb("zsp", [P, 4, 2, R64], F16)
        zs = sb("zs", [P, 2, T], F16)
        rb = sb("rb", [P, T])
        hid = sb("hid01", [P, 2, 2, 512])
        gv = [sb(f"gv_{i}", [P, 2, 2, 512], F16) for i in "hl"]
        uv = sb("uv", [P, 4, 2 * NE, RK])
        z2sp = sb("z2sp", [P, 2, 2, R64], F16)
        z2s = sb("z2s", [P, 2, P], F16)
        xoo = sb("xoo", [P, 4, D])
        mscr = nc.dram_tensor("mscr", (HB, P), F32, kind="Internal").ap()
        stage = [hid[:, :, :, :].rearrange("p a b c -> p (a b c)"), xoo[:, :, :].rearrange("p a b -> p (a b)")]

        ld_c = cnt("ld_c", 0)
        ld_x, ld_k, ld_v = cnt("ld_x", 16), cnt("ld_k", 16), cnt("ld_v", 16)
        ld_w = [cnt(f"ld_w{i}", 0) for i in range(2)]
        m_wr, m_bc, st_o = cnt("m_wr", 16), cnt("m_bc", 16), cnt("st_o", 16)
        passed = cnt("passed", 0)
        c_pool, c_dve, c_act = cnt("c_pool", 0), cnt("c_dve", 0), cnt("c_act", 0)
        w_hi, w_lo = cnt("w_hi", 0), cnt("w_lo", 0)
        cp_x, cp_k, cp_v = cnt("cp_x", 1), cnt("cp_k", 1), cnt("cp_v", 2)
        ln1, rs1, q_nd = cnt("ln1", 3), cnt("rs1", 2), cnt("q_nd", 2)
        qt_p, qt_s = cnt("qt_p", 2), cnt("qt_s", 2)
        gat_p, gat_s, gat_e, lf_d, lf_p = cnt("gat_p", 1), cnt("gat_s", 2), cnt("gat_e", 2), cnt("lf_d", 1), cnt("lf_p", 1)
        mx_d = cnt("mx_d", 4)
        em_a, em_p, em_s = cnt("em_a", 1), cnt("em_p", 1), cnt("em_s", 1)
        arg_d = cnt("arg_d", 2)
        arg_g, dec_a, dec_g = cnt("arg_g", 2), cnt("dec_a", 4), cnt("dec_g", 4)
        qk_p, c_d, c_hi, c_lo = cnt("qk_p", 8), cnt("c_d", 8), cnt("c_hi", 8), cnt("c_lo", 8)
        av_p, av_s = cnt("av_p", 4), cnt("av_s", 4)
        po_d, po_a, po_g = cnt("po_d", 9), cnt("po_a", 2), cnt("po_g", 1)
        ln2, rs2, xn_d = cnt("ln2", 3), cnt("rs2", 2), cnt("xn_d", 2)
        xt_p, xt_h, xt_l = cnt("xt_p", 2), cnt("xt_h", 2), cnt("xt_l", 2)
        ro_p, ro_d, ro_e, z_p, z_s = cnt("ro_p", 1), cnt("ro_d", 24), cnt("ro_e", 1), cnt("z_p", 2), cnt("z_s", 2)
        base_p, g0_a, del_p, g1_a = cnt("base_p", NS), cnt("g0_a", 2 * NS), cnt("del_p", NS), cnt("g1_a", 2 * NS)
        v_d_, g_d_, hi_a, lo_d = cnt("v_d", NS), cnt("g_d", NS), cnt("hi_a", 2 * NS), cnt("lo_d", 2 * NS)
        w2_p = cnt("w2_p", NS)
        z2_d, z2_p, z2_s, y_p, y_d = cnt("z2_d", 7), cnt("z2_p", 1), cnt("z2_s", 1), cnt("y_p", 1), cnt("y_d", 2)
        xo_d = cnt("xo_d", 3)

        block = ctx.enter_context(nc.Block())
        NCONST = 9
        jobs = []
        for c in range(DC):
            jobs.append(([(w1t[c * P:(c + 1) * P, :], 0, P, 0, FF)], [(0, FF, WS, [w[:, c, :] for w in w1])]))
        for c in range(4):
            n = FC // 4
            src = w2t[c * n * P:(c + 1) * n * P, :].rearrange("(k p) d -> p k d", p=P)
            jobs.append(([(src, 0, P, 0, n * D)],
                         [(0, n * D, WS, [w[:, c * n:(c + 1) * n, :].rearrange("p k d -> p (k d)") for w in w2])]))
        jobs.append(([(b1lo, 0, R64, 0, FF), (b1lo, R64, P, 0, FF)], [(0, FF, WS * LORA, [w[:, :] for w in b1w])]))
        o1 = FC * R64
        o2 = o1 + DC * AC
        jobs.append(([(a2t.rearrange("(k p) r -> p k r", p=P), 0, P, 0, o1),
                      (a1r.rearrange("(c p) r -> p c r", p=P), 0, P, o1, o2),
                      (b2lo, 0, R64, o2, o2 + D), (b2lo, R64, P, o2, o2 + D)],
                     [(0, o1, WS, [w[:, :, :].rearrange("p k r -> p (k r)") for w in a2]),
                      (o1, o2, WS, [w[:, :, :].rearrange("p k r -> p (k r)") for w in a1]),
                      (o2, o2 + D, WS * LORA, [w[:, :] for w in b2w])]))
        parts = [len(job[1]) for job in jobs]

        def bc2(ap):
            return ap.unsqueeze(1).to_broadcast([P, 2, ap.shape[1]])

        def unit(j):
            return decay[:, j // 2, 8 * (j % 2):8 * (j % 2) + 8, :]

        def a_of(j):
            return acol[:, 8 * j:8 * j + 8].unsqueeze(2).to_broadcast([P, 8, P])

        def steps(eng, body):
            body(-2)
            body(-1)
            body(0)
            with eng.Fori(1, NP - 2) as t:
                body(t)
            body(NP - 2)
            body(NP - 1)
            body(NP)

        def ok(n):
            return not isinstance(n, int) or 0 <= n < NP

        @block.sync
        def _(sp):
            def load(n):
                if past(n - 1):
                    sp.wait_ge(cp_x.sem, cp_x.at(n - 1, 1))
                if past(n - 1):
                    sp.wait_ge(q_nd.sem, q_nd.at(n - 1, 2))
                sp.dma_start(xin[:, :, :], x_d[n]).then_inc(ld_x.sem, 16)
                if past(n - 1):
                    sp.wait_ge(cp_k.sem, cp_k.at(n - 1, 1))
                if past(n - 1):
                    sp.wait_ge(gat_p.sem, gat_p.at(n - 1, 1))
                sp.dma_start(kin[:, :, :], k_d[n]).then_inc(ld_k.sem, 16)
                if past(n - 1):
                    sp.wait_ge(cp_v.sem, cp_v.at(n - 1, 2))
                sp.dma_start(vin[:, :, :], v_d[n]).then_inc(ld_v.sem, 16)

            def weights(j):
                if j >= 2:
                    sp.wait_ge(w_hi.sem, sum(parts[:j - 1]))
                    sp.wait_ge(w_lo.sem, sum(parts[:j - 1]))
                for src, p0, p1, c0, c1_ in jobs[j][0]:
                    dst = stage[j % 2][p0:p1, c0:c1_]
                    if len(src.shape) == 3:
                        dst = dst.rearrange("p (a b) -> p a b", b=src.shape[2])
                    sp.dma_start(dst, src).then_inc(ld_w[j % 2].sem, 16)

            def body(t):
                u_, m, p = t - 1, t + 1, t + 2
                if isinstance(t, int) and t == -2:
                    load(0)
                    sp.dma_start(wg[:, :, :], wgate).then_inc(ld_c.sem, 16)
                    sp.dma_start(bg[:, :], bgate.partition_broadcast(P)).then_inc(ld_c.sem, 16)
                    sp.dma_start(tg[:, 0:1], gx.partition_broadcast(P)).then_inc(ld_c.sem, 16)
                    sp.dma_start(tg[:, 1:2], gf.partition_broadcast(P)).then_inc(ld_c.sem, 16)
                    sp.dma_start(lnsg[:, :], lnscale.partition_broadcast(P)).then_inc(ld_c.sem, 16)
                    sp.dma_start(b2g[:, :], b2.partition_broadcast(P)).then_inc(ld_c.sem, 16)
                    sp.dma_start(brb[:, 0, :], br.partition_broadcast(P)).then_inc(ld_c.sem, 16)
                    sp.dma_start(brb[:, 1, :], br.partition_broadcast(P)).then_inc(ld_c.sem, 16)
                    sp.dma_start(b1s[:, :], b1c).then_inc(ld_c.sem, 16)
                    weights(0)
                    weights(1)
                    return
                if ok(m):
                    sp.wait_ge(mx_d.sem, mx_d.at(m, 3))
                    if past(m - 1):
                        sp.wait_ge(m_bc.sem, m_bc.at(m - 1, 16))
                    sp.dma_start(mscr, MT[:, :]).then_inc(m_wr.sem, 16)
                    sp.wait_ge(m_wr.sem, m_wr.at(m, 16))
                    if past(m - 1):
                        sp.wait_ge(c_d.sem, c_d.at(m - 1, 8))
                    sp.dma_start(decay[:, :, :, :].rearrange("p b h s -> p (b h s)"),
                                 mscr.rearrange("h s -> (h s)").partition_broadcast(P)).then_inc(m_bc.sem, 16)
                if ok(p):
                    load(p)
                if isinstance(t, int) and t == -1:
                    for j in range(2, len(jobs)):
                        weights(j)
                if ok(u_):
                    sp.wait_ge(y_d.sem, y_d.at(u_, 2))
                    sp.dma_start(o_d[u_], xoo[:, 2:4, :]).then_inc(st_o.sem, 16)
            steps(sp, body)
            sp.wait_ge(st_o.sem, 16 * NP)

        @block.gpsimd
        def _(pool):
            def body(t):
                m, p = t + 1, t + 2
                if isinstance(t, int) and t == -2:
                    for tile, v in ((ident, 0.0), (tri, 1.0), (ntri, -1.0), (mhalf, -0.5), (euler, 2.718281828459045)):
                        pool.memset(tile[:, :], v).then_inc(c_pool.sem, 1)
                    for part, v in ((vaug[0], 1.0), (vaug[1], 0.0)):
                        pool.memset(part[:, :, :, DH:DH + 1], v).then_inc(c_pool.sem, 1)
                    for e in range(NE):
                        pool.memset(rev[:, :, e:e + 1], float(NE - e)).then_inc(c_pool.sem, 1)
                    pool.wait_ge(c_pool.sem, 7 + NE)
                    pool.affine_select(out=ident[:, :], in_=ident[:, :], compare_op=ALU.not_equal, fill=1.0, base=0,
                                       pattern=[[-1, P]], channel_multiplier=1).then_inc(c_pool.sem, 1)
                    for tile in (tri, ntri):
                        pool.affine_select(out=tile[:, :], in_=tile[:, :], compare_op=ALU.is_ge, fill=0.0, base=0,
                                           pattern=[[1, P]], channel_multiplier=-1).then_inc(c_pool.sem, 1)
                    pool.wait_ge(c_pool.sem, 10 + NE)
                    pool.tensor_copy(identh[:, :], ident[:, :]).then_inc(c_pool.sem, 1)
                if ok(m):
                    if past(m - 1):
                        pool.wait_ge(po_d.sem, po_d.at(m - 1, 9))
                    apart(pool, m - 1, passed)
                    pool.wait_ge(ld_x.sem, ld_x.at(m, 16))
                    apart(pool, m, passed)
                    pool.tensor_copy(xres[:, :, :], xin[:, :, :]).then_inc(cp_x.sem, 1)
                    if past(m - 1):
                        pool.wait_ge(qk_p.sem, qk_p.at(m - 1, 8))
                    apart(pool, m - 1, passed)
                    pool.wait_ge(ld_k.sem, ld_k.at(m, 16))
                    apart(pool, m, passed)
                    pool.tensor_copy(kT[:, :, :], kin[:, :, :]).then_inc(cp_k.sem, 1)
                    if past(m - 1):
                        pool.wait_ge(av_p.sem, av_p.at(m - 1, 4))
                    apart(pool, m - 1, passed)
                    pool.wait_ge(ld_v.sem, ld_v.at(m, 16))
                    apart(pool, m, passed)
                    v4 = vin[:, :, :].rearrange("p b (h e) -> p b h e", e=DH)
                    pool.tensor_copy(vaug[0][:, :, :, 0:DH], v4).then_inc(cp_v.sem, 1)
                if ok(t):
                    pool.wait_ge(ro_d.sem, ro_d.at(t, 16))
                    apart(pool, t, passed)
                    pool.tensor_tensor(pe_[:, :], euler[:, :], ex[:, :], ALU.pow).then_inc(ro_e.sem, 1)
                if ok(m):
                    pool.wait_ge(cp_v.sem, cp_v.at(m, 1))
                    apart(pool, m, passed)
                    pool.tensor_tensor(vaug[1][:, :, :, 0:DH], v4, vaug[0][:, :, :, 0:DH], ALU.subtract)\
                        .then_inc(cp_v.sem, 1)
                    pool.wait_ge(m_bc.sem, m_bc.at(m, 16))
                    apart(pool, m, passed)
                    pool.wait_ge(mx_d.sem, mx_d.at(m, 4))
                    apart(pool, m, passed)
                    for j in (2, 3):
                        d = unit(j)
                        pool.tensor_tensor(d, a_of(j), d, ALU.subtract).then_inc(arg_g.sem, 1)
                    for j in range(4):
                        pool.wait_ge(dec_a.sem, dec_a.at(m, j + 1))
                        apart(pool, m, passed)
                        d = unit(j)
                        pool.affine_select(out=d, in_=d, compare_op=ALU.is_ge, fill=0.0, base=0,
                                           pattern=[[0, 8], [1, P]], channel_multiplier=-1).then_inc(dec_g.sem, 1)
                if ok(p):
                    pool.wait_ge(ln1.sem, ln1.at(p, 3))
                    apart(pool, p, passed)
                    pool.tensor_scalar(rv[:, 0, 0, :], bn[:, 0, :, 7], EPS_LN, None, ALU.add).then_inc(rs1.sem, 1)
                    pool.wait_ge(rs1.sem, rs1.at(p, 1))
                    apart(pool, p, passed)
                    pool.tensor_tensor(rv[:, 0, 1, :], rv[:, 0, 0, :], mhalf[:, 0:2], ALU.pow).then_inc(rs1.sem, 1)
                if ok(m):
                    pool.wait_ge(po_d.sem, po_d.at(m, 6))
                    apart(pool, m, passed)
                    pool.tensor_tensor(st[:, 5, :], st[:, 4, :], mhalf[:, :], ALU.pow).then_inc(po_g.sem, 1)
                    pool.wait_ge(ln2.sem, ln2.at(m, 3))
                    apart(pool, m, passed)
                    pool.tensor_scalar(rv[:, 1, 0, :], bn[:, 1, :, 7], EPS_LN, None, ALU.add).then_inc(rs2.sem, 1)
                    pool.wait_ge(rs2.sem, rs2.at(m, 1))
                    apart(pool, m, passed)
                    pool.tensor_tensor(rv[:, 1, 1, :], rv[:, 1, 0, :], mhalf[:, 0:2], ALU.pow).then_inc(rs2.sem, 1)
            steps(pool, body)

        @block.scalar
        def _(act):
            def gelu(n, i, second):
                done, src = (g1_a, del_p) if second else (g0_a, base_p)
                act.wait_ge(src.sem, src.at(n, i + 1))
                if not second:
                    prior = (n, i - 2) if i >= 2 else (n - 1, i - 2 + NS)
                    if past(prior[0]):
                        act.wait_ge(lo_d.sem, lo_d.at(prior[0], 2 * prior[1] + 2))
                for k in range(2):
                    act.activation(hid[:, int(second), i % 2, k * T:(k + 1) * T], H[i % 2][:, k * T:(k + 1) * T],
                                   ACT.Gelu_apprx_tanh, bias=b1s[:, 2 * i + k:2 * i + k + 1], scale=1.0 / WS)\
                        .then_inc(done.sem, 1)

            def evacuate(m, g):
                act.wait_ge(av_p.sem, av_p.at(m, g + 1))
                if g == 0 and past(m - 1):
                    act.wait_ge(po_d.sem, po_d.at(m - 1, 5))
                dst = u[:, (g // 2) * NH:(g // 2 + 1) * NH, :].rearrange("p (c q) e -> p q c e", q=4)
                act.activation(dst[:, 2 * (g % 2):2 * (g % 2) + 2],
                               G[:, 0:8 * (DH + 1)].rearrange("p (q c e) -> p q c e", q=2, c=4),
                               ACT.Copy).then_inc(av_s.sem, 1)

            def hi(n, i):
                act.wait_ge(v_d_.sem, v_d_.at(n, i + 1))
                prior = (n, i - 2) if i >= 2 else (n - 1, i - 2 + NS)
                if past(prior[0]):
                    act.wait_ge(w2_p.sem, w2_p.at(prior[0], prior[1] + 1))
                act.activation(gv[0][:, i % 2, 1, :], hid[:, 1, i % 2, :], ACT.Copy).then_inc(hi_a.sem, 1)
                act.wait_ge(g_d_.sem, g_d_.at(n, i + 1))
                act.activation(gv[0][:, i % 2, 0, :], hid[:, 0, i % 2, :], ACT.Copy).then_inc(hi_a.sem, 1)

            def c_high(m, r0):
                for r in (r0, r0 + 1):
                    act.wait_ge(c_d.sem, c_d.at(m, r + 1))
                    if r >= 4:
                        act.wait_ge(av_p.sem, av_p.at(m, r // 2 - 1))
                    elif past(m - 1):
                        act.wait_ge(av_p.sem, av_p.at(m - 1, r // 2 + 3))
                    act.activation(Cs[0][:, r % 4], Ct[:, r % 2], ACT.Copy).then_inc(c_hi.sem, 1)

            def weights(j):
                act.wait_ge(ld_w[j % 2].sem, 16 * sum(len(jobs[i][0]) for i in range(j % 2, j + 1, 2)))
                for c0, c1_, s, dst in jobs[j][1]:
                    act.activation(dst[0], stage[j % 2][:, c0:c1_], ACT.Copy, scale=s).then_inc(w_hi.sem, 1)

            def body(t):
                u_, m, p = t - 1, t + 1, t + 2
                if isinstance(t, int) and t == -2:
                    act.wait_ge(ld_c.sem, 16 * NCONST)
                    act.activation(tg[:, 2:4], tg[:, 0:2], ACT.Tanh).then_inc(c_act.sem, 1)
                if isinstance(t, int) and t == -1:
                    for j in range(2):
                        weights(j)
                for i in range(NS):
                    if i == 0:
                        if ok(u_):
                            gelu(u_, NS - 1, True)
                            hi(u_, NS - 1)
                        if ok(t):
                            act.wait_ge(z_p.sem, z_p.at(t, 1))
                            if past(t - 1):
                                act.wait_ge(del_p.sem, del_p.at(t - 1, NS))
                            act.activation(zs[:, :, :].rearrange("p a b -> p (a b)"),
                                           R[1][:, 0:T].bitcast(F16)[:, 0:2 * T], ACT.Copy).then_inc(z_s.sem, 1)
                    if i in (4, 5) and ok(m):
                        c_high(m, 4 * i - 14)
                    if i != 1 and ok(t):
                        gelu(t, i, False)
                    if i == 4 and ok(m):
                        evacuate(m, 0)
                    if i in (3, 4) and ok(m):
                        c_high(m, 4 * i - 12)
                    if i == 3 and ok(m):
                        act.wait_ge(em_p.sem, em_p.at(m, 1))
                        if past(m - 1):
                            act.wait_ge(po_d.sem, po_d.at(m - 1, 2))
                        act.activation(emt[:, :], G[:, 480:512], ACT.Copy).then_inc(em_s.sem, 1)
                    if i == 0 and ok(t):
                        act.wait_ge(z_p.sem, z_p.at(t, 2))
                        if past(t - 1):
                            act.wait_ge(v_d_.sem, v_d_.at(t - 1, NS))
                        act.activation(rb[:, :], R[1][:, T:2 * T], ACT.Copy).then_inc(z_s.sem, 1)
                    if i in (4, 5) and ok(m):
                        evacuate(m, 2 * i - 7)
                    if i >= 1 and ok(t):
                        gelu(t, i - 1, True)
                    if i == 1 and ok(t):
                        gelu(t, 1, False)
                    if i == 1 and ok(u_):
                        act.wait_ge(z2_p.sem, z2_p.at(u_, 1))
                        act.activation(z2s[:, :, :].rearrange("p a b -> p (a b)"),
                                       U[:, 256:384].bitcast(F16)[:, 0:T], ACT.Copy).then_inc(z2_s.sem, 1)
                    if i >= 1 and ok(t):
                        hi(t, i - 1)
                    if i == 2 and ok(m):
                        if past(m - 1):
                            act.wait_ge(em_p.sem, em_p.at(m - 1, 1))
                        act.wait_ge(mx_d.sem, mx_d.at(m, 4))
                        act.activation(em[:, :], FM[:, :], ACT.Exp, scale=-1.0).then_inc(em_a.sem, 1)
                        for j in range(4):
                            if j < 2:
                                act.wait_ge(arg_d.sem, arg_d.at(m, j + 1))
                            else:
                                act.wait_ge(arg_g.sem, arg_g.at(m, j - 1))
                            d = unit(j)
                            act.activation(d, d, ACT.Exp).then_inc(dec_a.sem, 1)
                    if i == 4 and ok(m):
                        evacuate(m, 2)
                    if i == 5 and ok(p):
                        for b in range(2):
                            act.wait_ge(qt_p.sem, qt_p.at(p, b + 1))
                            act.activation(qT[:, :, b, :], R[b][:, :].rearrange("p (c s) -> p c s", c=DC), ACT.Copy)\
                                .then_inc(qt_s.sem, 1)
                    if i == 5 and ok(m):
                        act.wait_ge(po_d.sem, po_d.at(m, 2))
                        act.activation(st[:, 2, :], st[:, 1, :], ACT.Square, bias=EPS ** 1.5, scale=EPS ** 0.5)\
                            .then_inc(po_a.sem, 1)
                        act.wait_ge(po_d.sem, po_d.at(m, 4))
                        act.activation(u[:, :, 0:DH], uc[:, :, :].rearrange("p b (h e) -> p (b h) e", e=DH), ACT.Square)\
                            .then_inc(po_a.sem, 1)
                    if i == 6 and ok(p):
                        act.wait_ge(gat_s.sem, gat_s.at(p, 2))
                        act.activation(gt[:, 1, :], gt[:, 0, :], ACT.Exp).then_inc(gat_e.sem, 1)
                        act.wait_ge(gat_e.sem, gat_e.at(p, 1))
                        act.activation(gt[:, 2, :], gt[:, 1, :], ACT.Ln, bias=1.0).then_inc(gat_e.sem, 1)
                    if isinstance(t, int) and t == -1:
                        weights(i + 2)
                if ok(m):
                    for b in range(2):
                        act.wait_ge(xt_p.sem, xt_p.at(m, b + 1))
                        if past(m - 1):
                            act.wait_ge(base_p.sem, base_p.at(m - 1, NS))
                        act.activation(xT[0][:, :, b * P:(b + 1) * P],
                                       R[b][:, :].rearrange("p (c s) -> p c s", c=DC), ACT.Copy).then_inc(xt_h.sem, 1)
            steps(act, body)

        @block.vector
        def _(dve):
            tt, ts, stt = dve.tensor_tensor, dve.tensor_scalar, dve.scalar_tensor_tensor

            def combine(n, i):
                h0, h1 = hid[:, 0, i % 2, :], hid[:, 1, i % 2, :]
                dve.wait_ge(g1_a.sem, g1_a.at(n, 2 * i + 2))
                if i == 0:
                    dve.wait_ge(z_s.sem, z_s.at(n, 2))
                pair = "p (k t) -> p k t"
                tt(h1.rearrange(pair, k=2), h1.rearrange(pair, k=2), bc2(rb[:, :]), ALU.mult).then_inc(v_d_.sem, 1)
                dve.wait_ge(v_d_.sem, v_d_.at(n, i + 1))
                tt(h0, h0, h1, ALU.add).then_inc(g_d_.sem, 1)
                dve.wait_ge(hi_a.sem, hi_a.at(n, 2 * i + 1))
                tt(gv[1][:, i % 2, 1, :], h1, gv[0][:, i % 2, 1, :], ALU.subtract).then_inc(lo_d.sem, 1)
                dve.wait_ge(g_d_.sem, g_d_.at(n, i + 1))
                dve.wait_ge(hi_a.sem, hi_a.at(n, 2 * i + 2))
                tt(gv[1][:, i % 2, 0, :], h0, gv[0][:, i % 2, 0, :], ALU.subtract).then_inc(lo_d.sem, 1)

            def decayed(m, r0):
                for r in (r0, r0 + 1):
                    dve.wait_ge(qk_p.sem, qk_p.at(m, r + 1))
                    dve.wait_ge(dec_g.sem, dec_g.at(m, 2 * (r // 4) + 2))
                    if r >= 2:
                        dve.wait_ge(c_lo.sem, c_lo.at(m, r - 1))
                    elif past(m - 1):
                        dve.wait_ge(c_lo.sem, c_lo.at(m - 1, r + 7))
                    d = decay[:, r // 4].rearrange("p (c q) s -> p q c s", q=4)[:, r % 4]
                    stt(Ct[:, r % 2], R[r % 2][:, :].rearrange("p (c s) -> p c s", c=4), SC, d,
                        ALU.mult, ALU.mult).then_inc(c_d.sem, 1)
                for r in (r0, r0 + 1):
                    dve.wait_ge(c_hi.sem, c_hi.at(m, r + 1))
                    tt(Cs[1][:, r % 4], Ct[:, r % 2], Cs[0][:, r % 4], ALU.subtract).then_inc(c_lo.sem, 1)

            def router(n, tail):
                first, second = rt[:, 2:2 + 2 * NE], rt[:, 2 + 2 * NE:2 + 4 * NE]
                oh0 = first.rearrange("p (b e) -> p b e", b=2)
                oh1 = second.rearrange("p (b e) -> p b e", b=2)
                k = [20 if tail else 0]

                def step(ins, fence=True):
                    ins.then_inc(ro_d.sem, 1)
                    k[0] += 1
                    if fence:
                        dve.wait_ge(ro_d.sem, ro_d.at(n, k[0]))

                def be(i):
                    return mx[:, i, :].unsqueeze(2).to_broadcast([P, 2, NE])

                if tail:
                    dve.wait_ge(ro_e.sem, ro_e.at(n, 1))
                    step(dve.tensor_reduce(mx[:, 4, :], pe_[:, 0:2 * NE].rearrange("p (b e) -> p b e", b=2), AX, ALU.add))
                    step(dve.reciprocal(mx[:, 5, :], mx[:, 4, :]))
                    step(ts(rt[:, 0:2], mx[:, 5, :], tg[:, 1:2], None, ALU.mult), False)
                    step(stt(c2[:, :], pe_[:, 2 * NE:2 * NE + 2], 1.0, mx[:, 5, :], ALU.add, ALU.mult))
                    assert k[0] == ro_d.per
                    return
                ps = R[0][:, 0:2 * AC].rearrange("p (b k) -> p b k", b=2)
                dve.wait_ge(ro_p.sem, ro_p.at(n, 1))
                step(ts(u1s[:, :, :].rearrange("p (b e) r -> p b (e r)", b=2), ps[:, :, 0:R64], 1.0 / WS, None, ALU.mult), False)
                step(stt(lg[:, :, :], ps[:, :, R64:AC], 1.0 / WS, brb[:, :, :], ALU.mult, ALU.add))
                step(dve.tensor_reduce(mx[:, 0, :], lg[:, :, :], AX, ALU.max))
                step(tt(eq[:, :, :], lg[:, :, :], be(0), ALU.is_equal))
                step(tt(eq[:, :, :], eq[:, :, :], rev[:, :, :], ALU.mult))
                step(dve.tensor_reduce(mx[:, 1, :], eq[:, :, :], AX, ALU.max))
                step(tt(oh0, eq[:, :, :], be(1), ALU.is_equal))
                step(stt(l2[:, :, :], oh0, -1e30, lg[:, :, :], ALU.mult, ALU.add))
                step(dve.tensor_reduce(mx[:, 2, :], l2[:, :, :], AX, ALU.max))
                step(tt(eq[:, :, :], l2[:, :, :], be(2), ALU.is_equal), False)
                step(tt(ex[:, 0:2 * NE].rearrange("p (b e) -> p b e", b=2), lg[:, :, :], be(0), ALU.subtract), False)
                step(tt(ex[:, 2 * NE:2 * NE + 2], mx[:, 2, :], mx[:, 0, :], ALU.subtract))
                step(tt(eq[:, :, :], eq[:, :, :], rev[:, :, :], ALU.mult))
                step(dve.tensor_reduce(mx[:, 3, :], eq[:, :, :], AX, ALU.max))
                step(tt(oh1, eq[:, :, :], be(3), ALU.is_equal))
                step(tt(ohd[:, :, :], oh1, oh0, ALU.subtract))
                for i, oh in enumerate((first, ohd[:, :, :].rearrange("p b e -> p (b e)"))):
                    step(tt(zf[:, i], u1s[:, :, :], oh.unsqueeze(2).to_broadcast([P, 2 * NE, RK]), ALU.mult), i == 1)
                zfv = zf[:, :, :, :].rearrange("p i (b e) r -> p (i b) (e r)", b=2)
                step(dve.tensor_copy(zsp[:, :, 0, :], zfv))
                step(tt(zsp[:, :, 1, :], zfv, zsp[:, :, 0, :], ALU.subtract))
                assert k[0] == 20

            def weights(j):
                done = sum(parts[:j])
                for i, (c0, c1_, s, dst) in enumerate(jobs[j][1]):
                    dve.wait_ge(w_hi.sem, done + i + 1)
                    stt(dst[1], stage[j % 2][:, c0:c1_], s, dst[0], ALU.mult, ALU.subtract).then_inc(w_lo.sem, 1)

            def body(t):
                u_, m, p = t - 1, t + 1, t + 2
                if isinstance(t, int) and t == -2:
                    dve.wait_ge(c_act.sem, 1)
                    ts(lnsg[:, :], lnsg[:, :], tg[:, 2:3], None, ALU.mult).then_inc(c_dve.sem, 1)
                    ts(b2g[:, :], b2g[:, :], tg[:, 3:4], None, ALU.mult).then_inc(c_dve.sem, 1)
                    ts(tg[:, 1:2], tg[:, 3:4], 1.0 / WS, None, ALU.mult).then_inc(c_dve.sem, 1)
                    tt(wg[:, DC:2 * DC, :], wg[:, DC:2 * DC, :], wg[:, 2 * DC:3 * DC, :], ALU.add).then_inc(c_dve.sem, 1)
                    dve.wait_ge(c_dve.sem, 4)
                if isinstance(t, int) and t == -1:
                    for j in range(2):
                        weights(j)
                for i in range(NS):
                    if i == 1 and ok(u_):
                        dve.wait_ge(w2_p.sem, w2_p.at(u_, NS))
                        uu = U[:, 0:256].rearrange("p (b k) -> p b k", b=2)
                        flat = "p (b e) r -> p b (e r)"
                        bce = [rtk[:, 2 + 2 * NE * c:2 + 2 * NE * (c + 1)].unsqueeze(2).to_broadcast([P, 2 * NE, RK])
                               for c in range(2)]
                        ts(uv[:, 0].rearrange(flat, b=2), uu[:, :, R64:2 * R64], 1.0 / WS, None, ALU.mult)\
                            .then_inc(z2_d.sem, 1)
                        dve.wait_ge(z2_d.sem, z2_d.at(u_, 1))
                        stt(uv[:, 1].rearrange(flat, b=2), uu[:, :, 0:R64], 1.0 / WS, uv[:, 0].rearrange(flat, b=2),
                            ALU.mult, ALU.subtract).then_inc(z2_d.sem, 1)
                        tt(uv[:, 2], uv[:, 0], bce[1], ALU.mult).then_inc(z2_d.sem, 1)
                        dve.wait_ge(z2_d.sem, z2_d.at(u_, 3))
                        tt(uv[:, 3], uv[:, 1], bce[0], ALU.mult).then_inc(z2_d.sem, 1)
                        dve.wait_ge(z2_d.sem, z2_d.at(u_, 4))
                        tt(uv[:, 0], uv[:, 2], uv[:, 3], ALU.add).then_inc(z2_d.sem, 1)
                        dve.wait_ge(z2_d.sem, z2_d.at(u_, 5))
                        dve.tensor_copy(z2sp[:, :, 0, :], uv[:, 0].rearrange(flat, b=2)).then_inc(z2_d.sem, 1)
                        dve.wait_ge(z2_d.sem, z2_d.at(u_, 6))
                        tt(z2sp[:, :, 1, :], uv[:, 0].rearrange(flat, b=2), z2sp[:, :, 0, :], ALU.subtract)\
                            .then_inc(z2_d.sem, 1)
                    if i == 2 and ok(u_):
                        dve.wait_ge(y_p.sem, y_p.at(u_, 1))
                        if past(u_ - 1):
                            dve.wait_ge(st_o.sem, st_o.at(u_ - 1, 16))
                        for b in range(2):
                            stt(xoo[:, 2 + b, :], Y[b][:, :], rtk[:, b:b + 1], xoo[:, b, :], ALU.mult, ALU.add)\
                                .then_inc(y_d.sem, 1)
                    if i == 2 and ok(m):
                        dve.wait_ge(mx_d.sem, mx_d.at(m, 4))
                        dve.wait_ge(m_bc.sem, m_bc.at(m, 16))
                        for j in range(2):
                            tt(unit(j), a_of(j), unit(j), ALU.subtract).then_inc(arg_d.sem, 1)
                    if i in (3, 4) and ok(m):
                        decayed(m, 4 * (i - 3))
                    if i == 5 and ok(m):
                        dve.wait_ge(av_s.sem, av_s.at(m, 4))
                        dve.wait_ge(em_s.sem, em_s.at(m, 1))
                        stt(st[:, 0, :], u[:, :, DH], -1.0, u[:, :, DH], ALU.mult, ALU.max).then_inc(po_d.sem, 1)
                        dve.wait_ge(po_d.sem, po_d.at(m, 1))
                        tt(st[:, 1, :], st[:, 0, :], emt[:, :], ALU.max).then_inc(po_d.sem, 1)
                        dve.tensor_reduce(st[:, 3, :], u[:, :, 0:DH], AX, ALU.add).then_inc(po_d.sem, 1)
                        dve.wait_ge(po_d.sem, po_d.at(m, 3))
                        if past(m - 1):
                            dve.wait_ge(xt_p.sem, xt_p.at(m - 1, 2))
                        ucv = uc[:, :, :].rearrange("p b (h e) -> p (b h) e", e=DH)
                        stt(ucv, st[:, 3, :].unsqueeze(2).to_broadcast([P, HB, DH]), -1.0 / DH, u[:, :, 0:DH],
                            ALU.mult, ALU.add).then_inc(po_d.sem, 1)
                    if i == 6 and ok(p):
                        dve.wait_ge(gat_p.sem, gat_p.at(p, 1))
                        tt(gb[:, :], G[:, 0:4 * NH], bg[:, :], ALU.add).then_inc(gat_s.sem, 1)
                        dve.wait_ge(gat_s.sem, gat_s.at(p, 1))
                        stt(gt[:, 0, :], gb[:, HB:], -1.0, gb[:, HB:], ALU.mult, ALU.min).then_inc(gat_s.sem, 1)
                    if i == 7 and ok(m):
                        dve.wait_ge(rs2.sem, rs2.at(m, 2))
                        for b in range(2):
                            ts(uc[:, b, :], x1[:, b, :], bn[:, 1, b, 6:7], rv[:, 1, 1, b:b + 1], ALU.subtract, ALU.mult)\
                                .then_inc(xn_d.sem, 1)
                    if i == 0:
                        if ok(u_):
                            combine(u_, NS - 1)
                        if ok(m):
                            dve.wait_ge(lf_p.sem, lf_p.at(m, 1))
                            dve.tensor_copy(aT[:, :], G[0:HB, 64:192]).then_inc(mx_d.sem, 1)
                            dve.wait_ge(mx_d.sem, mx_d.at(m, 1))
                            if past(m - 1):
                                dve.wait_ge(m_wr.sem, m_wr.at(m - 1, 16))
                            dve.tensor_tensor_scan(MT[:, :], aT[:, :], aT[:, :], -3.0e38, ALU.max, ALU.max)\
                                .then_inc(mx_d.sem, 1)
                            dve.wait_ge(mx_d.sem, mx_d.at(m, 2))
                            if past(m - 1):
                                dve.wait_ge(em_a.sem, em_a.at(m - 1, 1))
                            tt(FM[:, :], G[0:HB, 192:320], MT[:, :], ALU.add).then_inc(mx_d.sem, 1)
                            if past(m - 1):
                                dve.wait_ge(arg_g.sem, arg_g.at(m - 1, 2))
                            tt(acol[:, :], G[:, 320:352], gb[:, 0:HB], ALU.add).then_inc(mx_d.sem, 1)
                        if ok(t):
                            if isinstance(t, int) and t == 0:
                                dve.wait_ge(c_pool.sem, 11 + NE)
                            router(t, False)
                            router(t, True)
                    elif ok(t):
                        combine(t, i - 1)
                    if i == 3 and ok(t):
                        if past(t - 1):
                            dve.wait_ge(y_d.sem, y_d.at(t - 1, 2))
                        dve.tensor_copy(rtk[:, :], rt[:, :]).then_inc(xo_d.sem, 1)
                        for b in range(2):
                            stt(xoo[:, b, :], b2g[:, :], c2[:, b:b + 1], x1[:, b, :], ALU.mult, ALU.add)\
                                .then_inc(xo_d.sem, 1)
                    if i in (3, 4) and ok(m):
                        decayed(m, 4 * (i - 3) + 2)
                    if i == 3 and ok(p):
                        dve.wait_ge(ld_x.sem, ld_x.at(p, 16))
                        for b in range(2):
                            dve.bn_stats(bn[:, 0, b, 0:6], xin[:, b, :]).then_inc(ln1.sem, 1)
                        dve.wait_ge(ln1.sem, ln1.at(p, 2))
                        if past(p - 1):
                            dve.wait_ge(rs1.sem, rs1.at(p - 1, 2))
                        apart(dve, p - 1, passed)
                        dve.bn_aggr(bn[:, 0, 0, 6:8], bn[:, 0, 0, 0:6])
                        dve.bn_aggr(bn[:, 0, 1, 6:8], bn[:, 0, 1, 0:6]).then_inc(ln1.sem, 1)
                    if i == 4 and ok(p):
                        dve.wait_ge(rs1.sem, rs1.at(p, 2))
                        for b in range(2):
                            ts(qn[:, b, :], xin[:, b, :], bn[:, 0, b, 6:7], rv[:, 0, 1, b:b + 1], ALU.subtract, ALU.mult)\
                                .then_inc(q_nd.sem, 1)
                    if i == 5 and ok(m):
                        dve.wait_ge(po_a.sem, po_a.at(m, 2))
                        dve.tensor_reduce(st[:, 6, :], u[:, :, 0:DH], AX, ALU.add)\
                            .then_inc(po_d.sem, 1)
                        dve.wait_ge(po_d.sem, po_d.at(m, 5))
                        stt(st[:, 4, :], st[:, 6, :], 1.0 / DH, st[:, 2, :], ALU.mult, ALU.add).then_inc(po_d.sem, 1)
                    if i == 6 and ok(m):
                        dve.wait_ge(po_g.sem, po_g.at(m, 1))
                        tt(ucv, ucv, st[:, 5, :].unsqueeze(2).to_broadcast([P, HB, DH]), ALU.mult).then_inc(po_d.sem, 1)
                        dve.wait_ge(po_d.sem, po_d.at(m, 7))
                        tt(uc[:, :, :], uc[:, :, :], bc2(lnsg[:, :]), ALU.mult).then_inc(po_d.sem, 1)
                        dve.wait_ge(po_d.sem, po_d.at(m, 8))
                        tt(x1[:, :, :], uc[:, :, :], xres[:, :, :], ALU.add).then_inc(po_d.sem, 1)
                        dve.wait_ge(po_d.sem, po_d.at(m, 9))
                        for b in range(2):
                            dve.bn_stats(bn[:, 1, b, 0:6], x1[:, b, :]).then_inc(ln2.sem, 1)
                        dve.wait_ge(ln2.sem, ln2.at(m, 2))
                        apart(dve, m, passed)
                        dve.bn_aggr(bn[:, 1, 0, 6:8], bn[:, 1, 0, 0:6])
                        dve.bn_aggr(bn[:, 1, 1, 6:8], bn[:, 1, 1, 0:6]).then_inc(ln2.sem, 1)
                    if i == 7 and ok(p):
                        dve.wait_ge(gat_e.sem, gat_e.at(p, 2))
                        stt(gt[:, 3, :], gb[:, HB:], 0.0, gt[:, 2, :], ALU.min, ALU.subtract).then_inc(lf_d.sem, 1)
                    if isinstance(t, int) and t == -1:
                        weights(i + 2)
                if ok(m):
                    for b in range(2):
                        dve.wait_ge(xt_h.sem, xt_h.at(m, b + 1))
                        sl = slice(b * P, (b + 1) * P)
                        tt(xT[1][:, :, sl], R[b][:, :].rearrange("p (c s) -> p c s", c=DC), xT[0][:, :, sl],
                           ALU.subtract).then_inc(xt_l.sem, 1)
            steps(dve, body)

        @block.tensor
        def _(pe):
            def mm(out_, l, r, start, stop=False):
                return pe.matmul(out_, l, r, start=start, stop=stop, skip_group_check=True)

            def base(n, i):
                prior = (n, i - 2) if i >= 2 else (n - 1, i - 2 + NS)
                if past(prior[0]):
                    pe.wait_ge(g1_a.sem, g1_a.at(prior[0], 2 * prior[1] + 2))
                for k in range(2):
                    f = 2 * i + k
                    for c in range(DC):
                        for a, b in ((0, 0), (0, 1), (1, 0)):
                            mm(H[i % 2][:, k * T:(k + 1) * T], w1[a][:, c, f * P:(f + 1) * P], xT[b][:, c, :],
                               start=(k == 0 and c == 0 and a == 0 and b == 0))

            def lora(n, i, which, done):
                for k in range(2):
                    f = 2 * i + k
                    for a in range(2):
                        last = mm(H[i % 2][:, k * T:(k + 1) * T], b1w[a][:, f * P:(f + 1) * P], zs[:, which, :],
                                  start=False, stop=(a == 1))
                last.then_inc(done.sem, 1)

            def delta(n, i):
                pe.wait_ge(g0_a.sem, g0_a.at(n, 2 * i + 2))
                lora(n, i, 1, del_p)

            def lora2(i, k, b, what):
                f = 2 * i + k
                tok = slice(k * T + b * P, k * T + (b + 1) * P)
                uo = U[:, b * P + what * R64:b * P + (what + 1) * R64]
                for a, w in ((0, 0), (0, 1), (1, 0)):
                    l = gv[a][:, i % 2, what, tok]
                    last = mm(uo, l, a2[w][:, f, :],
                              start=(what == 1 and i == 0 and k == 0 and b == 0 and a == 0 and w == 0))
                    if what == 0:
                        last = mm(Y[b][:, :], l, w2[w][:, f, :], start=(i == 0 and k == 0 and a == 0 and w == 0))
                return last

            def piece(i, k, b):
                lora2(i, k, b, 1)
                return lora2(i, k, b, 0)

            def second(n, i):
                pe.wait_ge(lo_d.sem, lo_d.at(n, 2 * i + 1))
                for k in range(2):
                    for b in range(2):
                        lora2(i, k, b, 1)
                pe.wait_ge(lo_d.sem, lo_d.at(n, 2 * i + 2))
                if i == 0 and past(n - 1):
                    pe.wait_ge(y_d.sem, y_d.at(n - 1, 2))
                for k in range(2):
                    for b in range(2):
                        last = lora2(i, k, b, 0)
                last.then_inc(w2_p.sem, 1)

            def body(t):
                u_, m, p = t - 1, t + 1, t + 2
                if isinstance(t, int) and t == -2:
                    pe.wait_ge(c_pool.sem, 11 + NE)
                    pe.wait_ge(c_dve.sem, 4)
                if isinstance(t, int) and t == 0:
                    pe.wait_ge(w_hi.sem, sum(parts))
                    pe.wait_ge(w_lo.sem, sum(parts))
                for i in range(NS):
                    if ok(t) and i > 1:
                        base(t, i)
                        lora(t, i, 0, base_p)
                    if i == 2 and ok(u_):
                        pe.wait_ge(z2_d.sem, z2_d.at(u_, 7))
                        for b in range(2):
                            last = pe.transpose(U[:, 256 + b * R64:256 + (b + 1) * R64].bitcast(F16)[:, 0:P],
                                                z2sp[:, b].rearrange("p a r -> p (a r)"), identh[:, :])
                        last.then_inc(z2_p.sem, 1)
                    if i == 3 and ok(m):
                        pe.wait_ge(cp_k.sem, cp_k.at(m, 1))
                        apart(pe, m, passed)
                        pe.wait_ge(em_a.sem, em_a.at(m, 1))
                        apart(pe, m, passed)
                        pe.transpose(G[:, 480:512], em[:, :], ident[0:HB, 0:HB]).then_inc(em_p.sem, 1)
                    if i == 4 and ok(m):
                        products(m, 0)
                        scores(m, 4, t)
                        products(m, 1)
                    if i == 5 and ok(m):
                        products(m, 3)
                    if i == 5 and ok(p):
                        for b in range(2):
                            pe.wait_ge(q_nd.sem, q_nd.at(p, b + 1))
                            if ok(m):
                                pe.wait_ge(c_d.sem, c_d.at(m, 7 + b))
                            for c in range(DC):
                                last = pe.transpose(R[b][:, c * P:(c + 1) * P], qn[:, b, c * P:(c + 1) * P], ident[:, :])
                            last.then_inc(qt_p.sem, 1)
                    if i == 6 and ok(p):
                        if ok(m):
                            pe.wait_ge(av_s.sem, av_s.at(m, 4))
                        pe.wait_ge(ld_k.sem, ld_k.at(p, 16))
                        pe.wait_ge(qt_s.sem, qt_s.at(p, 2))
                        for b in range(2):
                            o = G[:, 0:4 * NH].rearrange("p (k b h) -> p k b h", k=2, b=2)[:, :, b, :]
                            for c in range(2 * DC):
                                l = qT[:, c, b, :] if c < DC else kin[:, c - DC, b * P:(b + 1) * P]
                                last = mm(o, l, wg[:, c, :].rearrange("p (k h) -> p k h", k=2), start=(c == 0),
                                          stop=(c == 2 * DC - 1))
                        last.then_inc(gat_p.sem, 1)
                    if i == 0:
                        if ok(u_):
                            delta(u_, NS - 1)
                            second(u_, NS - 2)
                        if ok(m):
                            pe.wait_ge(lf_d.sem, lf_d.at(m, 1))
                            lf = gt[:, 3, :]
                            mm(G[:, 320:352], ntri[:, :], lf, True, True)
                            mm(G[0:HB, 64:192], gb[:, 0:HB], ident[:, :], True)
                            mm(G[0:HB, 64:192], lf, ntri[:, :], False, True)
                            mm(G[0:HB, 192:320], lf, tri[:, :], True, True).then_inc(lf_p.sem, 1)
                        if ok(t):
                            pe.wait_ge(xt_l.sem, xt_l.at(t, 2))
                            for b in range(2):
                                for c in range(DC):
                                    for a, w in ((0, 0), (0, 1), (1, 0)):
                                        last = mm(R[0][:, b * AC:(b + 1) * AC], xT[a][:, c, b * P:(b + 1) * P],
                                                  a1[w][:, c, :], start=(c == 0 and a == 0 and w == 0),
                                                  stop=(c == DC - 1 and a == 1))
                            last.then_inc(ro_p.sem, 1)
                            base(t, 0)
                            base(t, 1)
                        if ok(u_):
                            pe.wait_ge(lo_d.sem, lo_d.at(u_, 2 * NS))
                            piece(NS - 1, 0, 0)
                        if ok(t):
                            pe.wait_ge(ro_d.sem, ro_d.at(t, 20))
                            for j in range(4):
                                last = pe.transpose(R[1][:, j * R64:(j + 1) * R64].bitcast(F16)[:, 0:P],
                                                    zsp[:, j].rearrange("p a r -> p (a r)"), identh[:, :])
                            last.then_inc(z_p.sem, 1)
                        if ok(u_):
                            piece(NS - 1, 0, 1)
                        if ok(t):
                            pe.wait_ge(z_s.sem, z_s.at(t, 1))
                            lora(t, 0, 0, base_p)
                            lora(t, 1, 0, base_p)
                            pe.wait_ge(ro_e.sem, ro_e.at(t, 1))
                            for b in range(2):
                                last = pe.transpose(R[1][:, T + b * P:T + (b + 1) * P],
                                                    pe_[:, 2 * NE + b:2 * NE + b + 1].to_broadcast([P, P]), ident[:, :])
                            last.then_inc(z_p.sem, 1)
                        if ok(u_):
                            piece(NS - 1, 1, 0)
                    elif i == 1:
                        if ok(t):
                            delta(t, 0)
                        if ok(u_):
                            piece(NS - 1, 1, 1).then_inc(w2_p.sem, 1)
                    else:
                        if ok(t):
                            delta(t, i - 1)
                        if i == 2 and ok(u_):
                            pe.wait_ge(z2_s.sem, z2_s.at(u_, 1))
                            for b in range(2):
                                for a in range(2):
                                    last = mm(Y[b][:, :], z2s[:, b, :], b2w[a][:, :], start=False, stop=(a == 1))
                            last.then_inc(y_p.sem, 1)
                        if i == 2 and ok(m):
                            pe.wait_ge(cp_k.sem, cp_k.at(m, 1))
                            scores(m, 0, t)
                        if ok(t):
                            second(t, i - 2)
                        if i == 7 and ok(m):
                            for b in range(2):
                                pe.wait_ge(xn_d.sem, xn_d.at(m, b + 1))
                                if ok(p):
                                    pe.wait_ge(qt_s.sem, qt_s.at(p, b + 1))
                                for c in range(DC):
                                    last = pe.transpose(R[b][:, c * P:(c + 1) * P], uc[:, b, c * P:(c + 1) * P], ident[:, :])
                                last.then_inc(xt_p.sem, 1)
                    if i == 3 and ok(m):
                        scores(m, 2, t)
                    if i == 4 and ok(m):
                        scores(m, 6, t)
                        products(m, 2)
            def scores(m, r0, t):
                for r in (r0, r0 + 1):
                    if r >= 2:
                        pe.wait_ge(c_d.sem, c_d.at(m, r - 1))
                    elif ok(t):
                        pe.wait_ge(ro_d.sem, ro_d.at(t, 2))
                        pe.wait_ge(z_s.sem, z_s.at(t, 2))
                    q, b = r % 4, r // 4
                    rows = slice(DH * q, DH * (q + 1))
                    for c in range(DC):
                        last = mm(R[r % 2][:, c * P:(c + 1) * P], kT[rows, c, b * P:(b + 1) * P], qT[rows, c, b, :],
                                  start=True, stop=True)
                    last.then_inc(qk_p.sem, 1)

            def products(m, g):
                if g == 0:
                    pe.wait_ge(em_s.sem, em_s.at(m, 1))
                    pe.wait_ge(cp_v.sem, cp_v.at(m, 2))
                else:
                    pe.wait_ge(av_s.sem, av_s.at(m, g))
                for r in (2 * g, 2 * g + 1):
                    pe.wait_ge(c_lo.sem, c_lo.at(m, r + 1))
                    for c in range(4):
                        o = ((r % 2) * 4 + c) * (DH + 1)
                        for a, w in ((0, 0), (0, 1), (1, 0)):
                            last = mm(G[:, o:o + DH + 1], Cs[a][:, r % 4, c, :], vaug[w][:, r // 4, 4 * c + r % 4, :],
                                      start=(a == 0 and w == 0), stop=(a == 1))
                last.then_inc(av_p.sem, 1)
            steps(pe, body)


def kernel(x, ctx_2048, g_xattn, g_ffn, L0_xattn_Wi, L0_xattn_bi, L0_xattn_Wf, L0_xattn_bf, L0_xattn_ln_scale,
           L0_ffn_W_r, L0_ffn_b_r, L0_ffn_W1, L0_ffn_b1, L0_ffn_W2, L0_ffn_b2, L0_ffn_A1, L0_ffn_B1, L0_ffn_A2,
           L0_ffn_B2):
    import numpy as np
    import concourse.bacc as bacc
    from concourse import mybir as mb
    from concourse.bass_utils import run_bass_kernel_spmd as run

    A = np.asarray
    nb, s, d = A(x).shape
    e, f, r = A(L0_ffn_B1).shape
    ctx = A(ctx_2048)
    wgate = np.concatenate([A(L0_xattn_Wi), A(L0_xattn_Wf)], axis=1)
    arrays = {
        "x": A(x),
        "ctx_tok": ctx,
        "ctx_T": ctx.reshape(nb // 2, 2 * s, d).transpose(0, 2, 1),
        "gx": A(g_xattn), "gf": A(g_ffn),
        "wgate": wgate.reshape(-1, 128, wgate.shape[1]).transpose(1, 0, 2),
        "bgate": np.concatenate([A(L0_xattn_bi)] * 2 + [A(L0_xattn_bf)] * 2),
        "lnscale": A(L0_xattn_ln_scale),
        "w1t": A(L0_ffn_W1).T, "w2t": A(L0_ffn_W2).T,
        "b1c": A(L0_ffn_b1).reshape(-1, 128).T, "b2": A(L0_ffn_b2),
        "a1r": np.concatenate([A(L0_ffn_A1).reshape(e * r, d).T, A(L0_ffn_W_r).T], axis=1),
        "br": A(L0_ffn_b_r),
        "b1lo": A(L0_ffn_B1).transpose(0, 2, 1).reshape(e * r, f),
        "a2t": A(L0_ffn_A2).reshape(e * r, f).T,
        "b2lo": A(L0_ffn_B2).transpose(0, 2, 1).reshape(e * r, d),
    }
    nc = bacc.Bacc("TRN2", target_bir_lowering=False, num_devices=1)
    ins, args = {}, []
    for name, a in arrays.items():
        a = np.ascontiguousarray(a)
        ins["in_" + name] = a
        args.append(nc.dram_tensor("in_" + name, a.shape, mb.dt.from_np(a.dtype), kind="ExternalInput").ap())
    args.append(nc.dram_tensor("out_0", A(x).shape, mb.dt.float32, kind="ExternalOutput").ap())
    flamingo_kernel(nc, *args)
    res = run(nc, [ins], core_ids=[0])
    return res.results[0]["out_0"]
```

```python
from contextlib import ExitStack

import concourse.bass as bass
from concourse import mybir

F32 = mybir.dt.float32
F16 = mybir.dt.float16
ALU = mybir.AluOpType
ACT = mybir.ActivationFunctionType
AX = mybir.AxisListType.X

P = 128
WS = 64.0
LORA = 2.0
EPS_LN = 1e-5
EPS = 1e-6


class Count:

    def __init__(self, sem, per):
        self.sem, self.per = sem, per

    def at(self, n, k):
        return n * self.per + k


def past(n):
    return not isinstance(n, int) or n >= 0


def apart(eng, n, passed):
    if not isinstance(n, int):
        eng.sem_inc(passed.sem)


def flamingo_kernel(nc, x, ctx_tok, ctx_T, gx, gf, wgate, bgate, lnscale, w1t, w2t, b1c, b2, a1r, br, b1lo, a2t, b2lo,
                    out):
    NB, S, D = x.shape
    NP = NB // 2
    DC = D // P
    NH = wgate.shape[2] // 2
    DH = D // NH
    FF = w1t.shape[1]
    FC = FF // P
    NS = FC // 2
    NE = br.shape[0]
    R64 = b1lo.shape[0]
    RK = R64 // NE
    T = 2 * S
    HB = 2 * NH
    NR = 8
    SC = float(DH) ** -0.5
    AC = R64 + NE
    assert S == P and NS == 8 and NH == 16 and DH == 32 and T * 2 == 512

    x_d = x.rearrange("(n b) s d -> n s b d", b=2)
    v_d = ctx_tok.rearrange("(n b) s d -> n s b d", b=2)
    k_d = ctx_T.rearrange("n (c p) t -> n p c t", p=P)
    o_d = out.rearrange("(n b) s d -> n s b d", b=2)

    with ExitStack() as ctx:
        def sb(name, shape, dt=F32):
            return ctx.enter_context(nc.sbuf_tensor(name, shape, dt))

        def cnt(name, per):
            return Count(ctx.enter_context(nc.semaphore(name)), per)

        Y = [ctx.enter_context(nc.psum_tensor(f"y{b}", [P, D], F32)) for b in range(2)]
        U = ctx.enter_context(nc.psum_tensor("u_lora", [P, 512], F32))
        H = [ctx.enter_context(nc.psum_tensor(f"hid{b}", [P, 512], F32)) for b in range(2)]
        R = [ctx.enter_context(nc.psum_tensor(f"ring{b}", [P, 512], F32)) for b in range(2)]
        G = ctx.enter_context(nc.psum_tensor("gates_av", [P, 512], F32))

        w1 = [sb(f"w1_{i}", [P, DC, FF], F16) for i in "hl"]
        w2 = [sb(f"w2_{i}", [P, FC, D], F16) for i in "hl"]
        b1w = [sb(f"b1w_{i}", [P, FF], F16) for i in "hl"]
        a2 = sb("a2", [P, FC, 2, R64], F16)
        a1 = [sb(f"a1_{i}", [P, DC, AC], F16) for i in "hl"]
        b2w = [sb(f"b2w_{i}", [P, D], F16) for i in "hl"]
        wgs = [sb(f"wg_{i}", [P, 2 * DC, 2 * NH], F16) for i in "hl"]
        b1s = sb("b1s", [P, FC])
        bg = sb("bg", [P, 4 * NH])
        lnsg = sb("lnsg", [P, D])
        b2g = sb("b2g", [P, D])
        brb = sb("brb", [P, 2, NE])
        tg = sb("tg", [P, 4])
        ident = sb("ident", [P, P])
        identh = sb("identh", [P, P], F16)
        tri = sb("tri", [P, P])
        ntri = sb("ntri", [P, P])
        rev = sb("rev", [P, 2, NE])
        mhalf = sb("mhalf", [P, HB])
        euler = sb("euler", [P, 2 * NE + 2])
        xin = sb("xin", [P, 2, D])
        xres = sb("xres", [P, 2, D])
        kin = sb("kin", [P, DC, T])
        kT = [sb(f"kT_{i}", [P, DC, T], F16) for i in "hl"]
        vin = sb("vin", [P, 2, D])
        vaug = [sb(f"vaug_{i}", [P, 2, NH, DH + 1], F16) for i in "hl"]
        qn = sb("qn", [P, 2, D])
        qT = [sb(f"qT_{i}", [P, DC, 2, P], F16) for i in "hl"]
        gb = sb("gb", [P, 4 * NH])
        gt = sb("gt", [P, 4, HB])
        aT = sb("aT", [HB, P])
        MT = sb("MT", [HB, P])
        FM = sb("FM", [HB, P])
        em = sb("em", [HB, P])
        emt = sb("emt", [P, HB])
        acol = sb("acol", [P, HB])
        decay = sb("decay", [P, 2, NH, P])
        Ct = sb("Ct", [P, 2, 4, P])
        Cs = [sb(f"C_{i}", [P, 4, 4, P], F16) for i in "hl"]
        u = sb("u", [P, HB, DH + 1])
        uc = sb("uc", [P, 2, D])
        st = sb("st", [P, 8, HB])
        bn = sb("bn", [P, 2, 2, 8])
        rv = sb("rv", [P, 2, 2, 2])
        x1 = sb("x1", [P, 2, D])
        xT = [sb(f"xT_{i}", [P, DC, T], F16) for i in "hl"]
        lg = sb("lg", [P, 2, NE])
        l2 = sb("l2", [P, 2, NE])
        eq = sb("eq", [P, 2, NE])
        mx = sb("mx", [P, 6, 2])
        ex = sb("ex", [P, 2 * NE + 2])
        pe_ = sb("pe_", [P, 2 * NE + 2])
        rt = sb("rt", [P, 2 + 4 * NE])
        rtk = sb("rtk", [P, 2 + 4 * NE])
        ohd = sb("ohd", [P, 2, NE])
        c2 = sb("c2", [P, 2])
        u1s = sb("u1s", [P, 2 * NE, RK])
        zf = sb("zf", [P, 2, 2 * NE, RK])
        zsp = sb("zsp", [P, 4, 2, R64], F16)
        zs = sb("zs", [P, 2, T], F16)
        rb = sb("rb", [P, T])
        hid = sb("hid01", [P, 2, 2, 512])
        gv = [sb(f"gv_{i}", [P, 2, 2, 512], F16) for i in "hl"]
        uv = sb("uv", [P, 4, 2 * NE, RK])
        wg = uv[:, :, :, :].rearrange("p a b c -> p (a b c)")[:, 0:3 * DC * 2 * NH].rearrange("p (c h) -> p c h", h=2 * NH)
        z2sp = sb("z2sp", [P, 2, 2, R64], F16)
        z2s = sb("z2s", [P, 2, P], F16)
        xoo = sb("xoo", [P, 4, D])
        mscr = nc.dram_tensor("mscr", (HB, P), F32, kind="Internal").ap()
        stage = [hid[:, :, :, :].rearrange("p a b c -> p (a b c)"), xoo[:, :, :].rearrange("p a b -> p (a b)"),
                 sb("stage", [P, FF])[:, :]]
        SB = len(stage)

        ld_c = cnt("ld_c", 0)
        ld_x, ld_k, ld_v = cnt("ld_x", 16), cnt("ld_k", 16), cnt("ld_v", 16)
        ld_w = [cnt(f"ld_w{i}", 0) for i in range(SB)]
        w_hi, w_lo = cnt("w_hi", 0), cnt("w_lo", 0)
        m_wr, m_bc, st_o = cnt("m_wr", 16), cnt("m_bc", 16), cnt("st_o", 16)
        passed = cnt("passed", 0)
        c_pool, c_dve, c_act = cnt("c_pool", 0), cnt("c_dve", 0), cnt("c_act", 0)
        cp_x, cp_k, cp_v = cnt("cp_x", 1), cnt("cp_k", 2), cnt("cp_v", 2)
        ln1, rs1, q_nd = cnt("ln1", 3), cnt("rs1", 2), cnt("q_nd", 2)
        qt_p, qt_h, qt_l = cnt("qt_p", 2), cnt("qt_h", 2), cnt("qt_l", 2)
        gat_p, gat_s, gat_e, lf_d, lf_p = cnt("gat_p", 1), cnt("gat_s", 2), cnt("gat_e", 2), cnt("lf_d", 1), cnt("lf_p", 1)
        mx_d = cnt("mx_d", 4)
        em_a, em_p, em_s = cnt("em_a", 1), cnt("em_p", 1), cnt("em_s", 1)
        arg_g, dec_a, dec_g = cnt("arg_g", 4), cnt("dec_a", 4), cnt("dec_g", 4)
        qk_p, c_d, c_hi, c_lo = cnt("qk_p", 8), cnt("c_d", 8), cnt("c_hi", 8), cnt("c_lo", 8)
        av_p, av_s = cnt("av_p", 4), cnt("av_s", 4)
        po_d = [cnt(f"po_d{b}", 9) for b in range(2)]
        po_a = [cnt(f"po_a{b}", 2) for b in range(2)]
        po_g = [cnt(f"po_g{b}", 1) for b in range(2)]
        ln2, rs2, xn_d = cnt("ln2", 3), cnt("rs2", 2), cnt("xn_d", 2)
        xt_p, xt_h, xt_l = cnt("xt_p", 2), cnt("xt_h", 2), cnt("xt_l", 2)
        ro_p, ro_d, ro_e, z_p, z_s = cnt("ro_p", 1), cnt("ro_d", 24), cnt("ro_e", 1), cnt("z_p", 2), cnt("z_s", 2)
        base_p, g0_a, del_p, g1_a = cnt("base_p", NS), cnt("g0_a", 2 * NS), cnt("del_p", NS), cnt("g1_a", 2 * NS)
        v_d_, g_d_, hi_a, lo_d = cnt("v_d", NS), cnt("g_d", NS), cnt("hi_a", 2 * NS), cnt("lo_d", 2 * NS)
        w2_p = cnt("w2_p", NS)
        z2_d, z2_p, z2_s, y_p, y_d = cnt("z2_d", 8), cnt("z2_p", 1), cnt("z2_s", 1), cnt("y_p", 1), cnt("y_d", 2)
        xo_d = cnt("xo_d", 3)

        block = ctx.enter_context(nc.Block())
        NCONST = 9
        jobs = []
        for c in range(DC):
            jobs.append(([(w1t[c * P:(c + 1) * P, :], 0, P, 0, FF)], [(0, FF, WS, [w[:, c, :] for w in w1])]))
        for c in range(4):
            n = FC // 4
            src = w2t[c * n * P:(c + 1) * n * P, :].rearrange("(k p) d -> p k d", p=P)
            jobs.append(([(src, 0, P, 0, n * D)],
                         [(0, n * D, WS, [w[:, c * n:(c + 1) * n, :].rearrange("p k d -> p (k d)") for w in w2])]))
        o1 = FC * R64
        o2 = o1 + DC * AC
        jobs.append(([(a2t.rearrange("(k p) r -> p k r", p=P), 0, P, 0, o1),
                      (a1r.rearrange("(c p) r -> p c r", p=P), 0, P, o1, o2),
                      (b2lo, 0, R64, o2, o2 + D), (b2lo, R64, P, o2, o2 + D)],
                     [(0, o1, WS, [a2[:, :, i, :] for i in range(2)]),
                      (o1, o2, WS, [w[:, :, :].rearrange("p k r -> p (k r)") for w in a1]),
                      (o2, o2 + D, WS * LORA, [w[:, :] for w in b2w])]))
        jobs.append(([(b1lo, 0, R64, 0, FF), (b1lo, R64, P, 0, FF)], [(0, FF, WS * LORA, [w[:, :] for w in b1w])]))
        parts = [len(job[1]) for job in jobs]
        WSLOT = {(-2, 5): (0,), (-2, 6): (1,), (-1, 0): (2, 3), (-1, 1): (4,), (-1, 2): (5, 6), (-1, 5): (7,),
                 (-1, 6): (8,), (-1, 7): (9,)}

        def staged(j, c0, c1_, dst):
            v = stage[j % SB][:, c0:c1_]
            return v if len(dst[0].shape) == 2 else v.rearrange("p (k r) -> p k r", r=dst[0].shape[2])

        def bc2(ap):
            return ap.unsqueeze(1).to_broadcast([P, 2, ap.shape[1]])

        def unit(j):
            return decay[:, j // 2, 8 * (j % 2):8 * (j % 2) + 8, :]

        def a_of(j):
            return acol[:, 8 * j:8 * j + 8].unsqueeze(2).to_broadcast([P, 8, P])

        def steps(eng, body):
            body(-2)
            body(-1)
            body(0)
            with eng.Fori(1, NP - 2) as t:
                body(t)
            body(NP - 2)
            body(NP - 1)
            body(NP)

        def ok(n):
            return not isinstance(n, int) or 0 <= n < NP

        @block.sync
        def _(sp):
            def load(n):
                if past(n - 1):
                    sp.wait_ge(cp_x.sem, cp_x.at(n - 1, 1))
                if past(n - 1):
                    sp.wait_ge(q_nd.sem, q_nd.at(n - 1, 2))
                sp.dma_start(xin[:, :, :], x_d[n]).then_inc(ld_x.sem, 16)
                if past(n - 1):
                    sp.wait_ge(cp_k.sem, cp_k.at(n - 1, 2))
                sp.dma_start(kin[:, :, :], k_d[n]).then_inc(ld_k.sem, 16)
                if past(n - 1):
                    sp.wait_ge(cp_v.sem, cp_v.at(n - 1, 2))
                sp.dma_start(vin[:, :, :], v_d[n]).then_inc(ld_v.sem, 16)

            def weights(j):
                if j >= SB:
                    sp.wait_ge(w_hi.sem, sum(parts[:j - SB + 1]))
                    sp.wait_ge(w_lo.sem, sum(parts[:j - SB + 1]))
                for src, p0, p1, c0, c1_ in jobs[j][0]:
                    dst = stage[j % SB][p0:p1, c0:c1_]
                    if len(src.shape) == 3:
                        dst = dst.rearrange("p (a b) -> p a b", b=src.shape[2])
                    sp.dma_start(dst, src).then_inc(ld_w[j % SB].sem, 16)

            def body(t):
                u_, m, p = t - 1, t + 1, t + 2
                if isinstance(t, int) and t == -2:
                    load(0)
                    sp.dma_start(wg, wgate).then_inc(ld_c.sem, 16)
                    sp.dma_start(bg[:, :], bgate.partition_broadcast(P)).then_inc(ld_c.sem, 16)
                    sp.dma_start(tg[:, 0:1], gx.partition_broadcast(P)).then_inc(ld_c.sem, 16)
                    sp.dma_start(tg[:, 1:2], gf.partition_broadcast(P)).then_inc(ld_c.sem, 16)
                    sp.dma_start(lnsg[:, :], lnscale.partition_broadcast(P)).then_inc(ld_c.sem, 16)
                    sp.dma_start(b2g[:, :], b2.partition_broadcast(P)).then_inc(ld_c.sem, 16)
                    sp.dma_start(brb[:, 0, :], br.partition_broadcast(P)).then_inc(ld_c.sem, 16)
                    sp.dma_start(brb[:, 1, :], br.partition_broadcast(P)).then_inc(ld_c.sem, 16)
                    sp.dma_start(b1s[:, :], b1c).then_inc(ld_c.sem, 16)
                    for j in range(5):
                        weights(j)
                    return
                if ok(m):
                    sp.wait_ge(mx_d.sem, mx_d.at(m, 3))
                    if past(m - 1):
                        sp.wait_ge(m_bc.sem, m_bc.at(m - 1, 16))
                    sp.dma_start(mscr, MT[:, :]).then_inc(m_wr.sem, 16)
                    sp.wait_ge(m_wr.sem, m_wr.at(m, 16))
                    if past(m - 1):
                        sp.wait_ge(c_d.sem, c_d.at(m - 1, 8))
                    sp.dma_start(decay[:, :, :, :].rearrange("p b h s -> p (b h s)"),
                                 mscr.rearrange("h s -> (h s)").partition_broadcast(P)).then_inc(m_bc.sem, 16)
                if ok(p):
                    load(p)
                if isinstance(t, int) and t == -1:
                    for j in range(5, len(jobs)):
                        weights(j)
                if ok(u_):
                    sp.wait_ge(y_d.sem, y_d.at(u_, 2))
                    sp.dma_start(o_d[u_], xoo[:, 2:4, :]).then_inc(st_o.sem, 16)
            steps(sp, body)
            sp.wait_ge(st_o.sem, 16 * NP)

        @block.gpsimd
        def _(pool):
            def body(t):
                m, p = t + 1, t + 2
                if isinstance(t, int) and t == -2:
                    for tile, v in ((ident, 0.0), (tri, 1.0), (ntri, -1.0), (mhalf, -0.5), (euler, 2.718281828459045)):
                        pool.memset(tile[:, :], v).then_inc(c_pool.sem, 1)
                    for part, v in ((vaug[0], 1.0), (vaug[1], 0.0)):
                        pool.memset(part[:, :, :, DH:DH + 1], v).then_inc(c_pool.sem, 1)
                    for e in range(NE):
                        pool.memset(rev[:, :, e:e + 1], float(NE - e)).then_inc(c_pool.sem, 1)
                    pool.wait_ge(c_pool.sem, 7 + NE)
                    pool.affine_select(out=ident[:, :], in_=ident[:, :], compare_op=ALU.not_equal, fill=1.0, base=0,
                                       pattern=[[-1, P]], channel_multiplier=1).then_inc(c_pool.sem, 1)
                    for tile in (tri, ntri):
                        pool.affine_select(out=tile[:, :], in_=tile[:, :], compare_op=ALU.is_ge, fill=0.0, base=0,
                                           pattern=[[1, P]], channel_multiplier=-1).then_inc(c_pool.sem, 1)
                    pool.wait_ge(c_pool.sem, 10 + NE)
                    pool.tensor_copy(identh[:, :], ident[:, :]).then_inc(c_pool.sem, 1)
                if ok(m):
                    if past(m - 1):
                        pool.wait_ge(po_d[1].sem, po_d[1].at(m - 1, 9))
                    apart(pool, m - 1, passed)
                    pool.wait_ge(ld_x.sem, ld_x.at(m, 16))
                    apart(pool, m, passed)
                    pool.tensor_copy(xres[:, :, :], xin[:, :, :]).then_inc(cp_x.sem, 1)
                    if past(m - 1):
                        pool.wait_ge(av_p.sem, av_p.at(m - 1, 4))
                    apart(pool, m - 1, passed)
                    pool.wait_ge(ld_v.sem, ld_v.at(m, 16))
                    apart(pool, m, passed)
                    v4 = vin[:, :, :].rearrange("p b (h e) -> p b h e", e=DH)
                    pool.tensor_copy(vaug[0][:, :, :, 0:DH], v4).then_inc(cp_v.sem, 1)
                if ok(t):
                    pool.wait_ge(ro_d.sem, ro_d.at(t, 16))
                    apart(pool, t, passed)
                    pool.tensor_tensor(pe_[:, :], euler[:, :], ex[:, :], ALU.pow).then_inc(ro_e.sem, 1)
                if ok(m):
                    pool.wait_ge(cp_v.sem, cp_v.at(m, 1))
                    apart(pool, m, passed)
                    pool.tensor_tensor(vaug[1][:, :, :, 0:DH], v4, vaug[0][:, :, :, 0:DH], ALU.subtract)\
                        .then_inc(cp_v.sem, 1)
                    pool.wait_ge(m_bc.sem, m_bc.at(m, 16))
                    apart(pool, m, passed)
                    pool.wait_ge(mx_d.sem, mx_d.at(m, 4))
                    apart(pool, m, passed)
                    for j in range(4):
                        d = unit(j)
                        pool.tensor_tensor(d, a_of(j), d, ALU.subtract).then_inc(arg_g.sem, 1)
                if ok(p):
                    pool.wait_ge(ln1.sem, ln1.at(p, 3))
                    apart(pool, p, passed)
                    pool.tensor_scalar(rv[:, 0, 0, :], bn[:, 0, :, 7], EPS_LN, None, ALU.add).then_inc(rs1.sem, 1)
                    pool.wait_ge(rs1.sem, rs1.at(p, 1))
                    apart(pool, p, passed)
                    pool.tensor_tensor(rv[:, 0, 1, :], rv[:, 0, 0, :], mhalf[:, 0:2], ALU.pow).then_inc(rs1.sem, 1)
                if ok(m):
                    for j in range(4):
                        pool.wait_ge(dec_a.sem, dec_a.at(m, j + 1))
                        apart(pool, m, passed)
                        d = unit(j)
                        pool.affine_select(out=d, in_=d, compare_op=ALU.is_ge, fill=0.0, base=0,
                                           pattern=[[0, 8], [1, P]], channel_multiplier=-1).then_inc(dec_g.sem, 1)
                if ok(p):
                    if past(p - 1):
                        pool.wait_ge(qk_p.sem, qk_p.at(p - 1, 8))
                    apart(pool, p - 1, passed)
                    pool.wait_ge(ld_k.sem, ld_k.at(p, 16))
                    apart(pool, p, passed)
                    pool.tensor_copy(kT[0][:, :, :], kin[:, :, :]).then_inc(cp_k.sem, 1)
                    pool.wait_ge(cp_k.sem, cp_k.at(p, 1))
                    apart(pool, p, passed)
                    pool.tensor_tensor(kT[1][:, :, :], kin[:, :, :], kT[0][:, :, :], ALU.subtract).then_inc(cp_k.sem, 1)
                if ok(m):
                    for b in range(2):
                        pool.wait_ge(po_d[b].sem, po_d[b].at(m, 6))
                        apart(pool, m, passed)
                        hs = slice(b * NH, (b + 1) * NH)
                        pool.tensor_tensor(st[:, 5, hs], st[:, 4, hs], mhalf[:, hs], ALU.pow).then_inc(po_g[b].sem, 1)
                    pool.wait_ge(ln2.sem, ln2.at(m, 3))
                    apart(pool, m, passed)
                    pool.tensor_scalar(rv[:, 1, 0, :], bn[:, 1, :, 7], EPS_LN, None, ALU.add).then_inc(rs2.sem, 1)
                    pool.wait_ge(rs2.sem, rs2.at(m, 1))
                    apart(pool, m, passed)
                    pool.tensor_tensor(rv[:, 1, 1, :], rv[:, 1, 0, :], mhalf[:, 0:2], ALU.pow).then_inc(rs2.sem, 1)
            steps(pool, body)

        @block.scalar
        def _(act):
            def gelu(n, i, second):
                done, src = (g1_a, del_p) if second else (g0_a, base_p)
                act.wait_ge(src.sem, src.at(n, i + 1))
                if not second:
                    prior = (n, i - 2) if i >= 2 else (n - 1, i - 2 + NS)
                    if past(prior[0]):
                        act.wait_ge(lo_d.sem, lo_d.at(prior[0], 2 * prior[1] + 2))
                for k in range(2):
                    act.activation(hid[:, int(second), i % 2, k * T:(k + 1) * T], H[i % 2][:, k * T:(k + 1) * T],
                                   ACT.Gelu_apprx_tanh, bias=b1s[:, 2 * i + k:2 * i + k + 1], scale=1.0 / WS)\
                        .then_inc(done.sem, 1)

            def evacuate(m, g):
                act.wait_ge(av_p.sem, av_p.at(m, g + 1))
                if g % 2 == 0 and past(m - 1):
                    act.wait_ge(po_d[g // 2].sem, po_d[g // 2].at(m - 1, 5))
                dst = u[:, (g // 2) * NH:(g // 2 + 1) * NH, :].rearrange("p (c q) e -> p q c e", q=4)
                act.activation(dst[:, 2 * (g % 2):2 * (g % 2) + 2],
                               G[:, 0:8 * (DH + 1)].rearrange("p (q c e) -> p q c e", q=2, c=4),
                               ACT.Copy).then_inc(av_s.sem, 1)

            def hi(n, i):
                act.wait_ge(v_d_.sem, v_d_.at(n, i + 1))
                prior = (n, i - 2) if i >= 2 else (n - 1, i - 2 + NS)
                if past(prior[0]):
                    act.wait_ge(w2_p.sem, w2_p.at(prior[0], prior[1] + 1))
                act.activation(gv[0][:, i % 2, 1, :], hid[:, 1, i % 2, :], ACT.Copy).then_inc(hi_a.sem, 1)
                act.wait_ge(g_d_.sem, g_d_.at(n, i + 1))
                act.activation(gv[0][:, i % 2, 0, :], hid[:, 0, i % 2, :], ACT.Copy).then_inc(hi_a.sem, 1)

            def squares(m, b):
                hs = slice(b * NH, (b + 1) * NH)
                act.wait_ge(po_d[b].sem, po_d[b].at(m, 2))
                act.activation(st[:, 2, hs], st[:, 1, hs], ACT.Square, bias=EPS ** 1.5, scale=EPS ** 0.5)\
                    .then_inc(po_a[b].sem, 1)
                act.wait_ge(po_d[b].sem, po_d[b].at(m, 4))
                act.activation(u[:, hs, 0:DH], uc[:, b, :].rearrange("p (h e) -> p h e", e=DH), ACT.Square)\
                    .then_inc(po_a[b].sem, 1)

            def decays(m, j0):
                for j in (j0, j0 + 1):
                    act.wait_ge(arg_g.sem, arg_g.at(m, j + 1))
                    act.activation(unit(j), unit(j), ACT.Exp).then_inc(dec_a.sem, 1)

            def c_high(m, r0):
                for r in (r0, r0 + 1):
                    act.wait_ge(c_d.sem, c_d.at(m, r + 1))
                    if r >= 4:
                        act.wait_ge(av_p.sem, av_p.at(m, r // 2 - 1))
                    elif past(m - 1):
                        act.wait_ge(av_p.sem, av_p.at(m - 1, r // 2 + 3))
                    act.activation(Cs[0][:, r % 4], Ct[:, r % 2], ACT.Copy).then_inc(c_hi.sem, 1)

            def weights(j):
                act.wait_ge(ld_w[j % SB].sem, 16 * sum(len(jobs[i][0]) for i in range(j % SB, j + 1, SB)))
                for c0, c1_, s, dst in jobs[j][1]:
                    act.activation(dst[0], staged(j, c0, c1_, dst), ACT.Copy, scale=s).then_inc(w_hi.sem, 1)

            def body(t):
                u_, m, p = t - 1, t + 1, t + 2
                if isinstance(t, int) and t == -2:
                    act.wait_ge(ld_c.sem, 16 * NCONST)
                    act.activation(tg[:, 2:4], tg[:, 0:2], ACT.Tanh).then_inc(c_act.sem, 1)
                for i in range(NS):
                    if i == 0:
                        if ok(u_):
                            gelu(u_, NS - 1, True)
                            hi(u_, NS - 1)
                        if ok(t):
                            act.wait_ge(z_p.sem, z_p.at(t, 1))
                            if past(t - 1):
                                act.wait_ge(del_p.sem, del_p.at(t - 1, NS))
                            act.activation(zs[:, :, :].rearrange("p a b -> p (a b)"),
                                           R[1][:, 0:T].bitcast(F16)[:, 0:2 * T], ACT.Copy).then_inc(z_s.sem, 1)
                    if i == 4 and ok(m):
                        c_high(m, 2)
                    if i != 1 and ok(t):
                        gelu(t, i, False)
                    if i == 4 and ok(m):
                        evacuate(m, 0)
                    if i == 4 and ok(m):
                        c_high(m, 4)
                    if i == 3 and ok(m):
                        c_high(m, 0)
                        act.wait_ge(em_p.sem, em_p.at(m, 1))
                        if past(m - 1):
                            act.wait_ge(po_d[1].sem, po_d[1].at(m - 1, 2))
                        act.activation(emt[:, :], G[:, 480:512], ACT.Copy).then_inc(em_s.sem, 1)
                    if i == 0 and ok(t):
                        act.wait_ge(z_p.sem, z_p.at(t, 2))
                        if past(t - 1):
                            act.wait_ge(v_d_.sem, v_d_.at(t - 1, NS))
                        act.activation(rb[:, :], R[1][:, T:2 * T], ACT.Copy).then_inc(z_s.sem, 1)
                    if i in (4, 5) and ok(m):
                        evacuate(m, 2 * i - 7)
                    if i >= 1 and ok(t):
                        gelu(t, i - 1, True)
                    if i == 1 and ok(t):
                        gelu(t, 1, False)
                    if i == 1 and ok(u_):
                        act.wait_ge(z2_p.sem, z2_p.at(u_, 1))
                        act.activation(z2s[:, :, :].rearrange("p a b -> p (a b)"),
                                       R[0][:, 0:2 * R64].bitcast(F16)[:, 0:T], ACT.Copy).then_inc(z2_s.sem, 1)
                    if i == 5 and ok(p):
                        for b in range(2):
                            act.wait_ge(qt_p.sem, qt_p.at(p, b + 1))
                            act.activation(qT[0][:, :, b, :], R[b][:, :].rearrange("p (c s) -> p c s", c=DC), ACT.Copy)\
                                .then_inc(qt_h.sem, 1)
                    if i == 5 and ok(m):
                        squares(m, 1)
                    if i == 4 and ok(m):
                        c_high(m, 6)
                        evacuate(m, 2)
                        squares(m, 0)
                    if i == 2 and ok(m):
                        decays(m, 0)
                    if i >= 1 and ok(t):
                        hi(t, i - 1)
                    if i == 2 and ok(m):
                        if past(m - 1):
                            act.wait_ge(em_p.sem, em_p.at(m - 1, 1))
                        act.wait_ge(mx_d.sem, mx_d.at(m, 4))
                        act.activation(em[:, :], FM[:, :], ACT.Exp, scale=-1.0).then_inc(em_a.sem, 1)
                        decays(m, 2)
                    if i == 6 and ok(p):
                        act.wait_ge(gat_s.sem, gat_s.at(p, 2))
                        act.activation(gt[:, 1, :], gt[:, 0, :], ACT.Exp).then_inc(gat_e.sem, 1)
                        act.wait_ge(gat_e.sem, gat_e.at(p, 1))
                        act.activation(gt[:, 2, :], gt[:, 1, :], ACT.Ln, bias=1.0).then_inc(gat_e.sem, 1)
                    if isinstance(t, int) and t < 0:
                        for j in WSLOT.get((t, i), ()):
                            weights(j)
                if ok(m):
                    for b in range(2):
                        act.wait_ge(xt_p.sem, xt_p.at(m, b + 1))
                        if past(m - 1):
                            act.wait_ge(base_p.sem, base_p.at(m - 1, NS))
                        act.activation(xT[0][:, :, b * P:(b + 1) * P],
                                       R[b][:, :].rearrange("p (c s) -> p c s", c=DC), ACT.Copy).then_inc(xt_h.sem, 1)
            steps(act, body)

        @block.vector
        def _(dve):
            tt, ts, stt = dve.tensor_tensor, dve.tensor_scalar, dve.scalar_tensor_tensor

            def combine(n, i):
                h0, h1 = hid[:, 0, i % 2, :], hid[:, 1, i % 2, :]
                dve.wait_ge(g1_a.sem, g1_a.at(n, 2 * i + 2))
                if i == 0:
                    dve.wait_ge(z_s.sem, z_s.at(n, 2))
                pair = "p (k t) -> p k t"
                tt(h1.rearrange(pair, k=2), h1.rearrange(pair, k=2), bc2(rb[:, :]), ALU.mult).then_inc(v_d_.sem, 1)
                dve.wait_ge(v_d_.sem, v_d_.at(n, i + 1))
                tt(h0, h0, h1, ALU.add).then_inc(g_d_.sem, 1)
                dve.wait_ge(hi_a.sem, hi_a.at(n, 2 * i + 1))
                tt(gv[1][:, i % 2, 1, :], h1, gv[0][:, i % 2, 1, :], ALU.subtract).then_inc(lo_d.sem, 1)
                dve.wait_ge(g_d_.sem, g_d_.at(n, i + 1))
                dve.wait_ge(hi_a.sem, hi_a.at(n, 2 * i + 2))
                tt(gv[1][:, i % 2, 0, :], h0, gv[0][:, i % 2, 0, :], ALU.subtract).then_inc(lo_d.sem, 1)

            def decayed(m, r0):
                for r in (r0, r0 + 1):
                    dve.wait_ge(qk_p.sem, qk_p.at(m, r + 1))
                    dve.wait_ge(dec_g.sem, dec_g.at(m, 2 * (r // 4) + 2))
                    if r >= 2:
                        dve.wait_ge(c_lo.sem, c_lo.at(m, r - 1))
                    elif past(m - 1):
                        dve.wait_ge(c_lo.sem, c_lo.at(m - 1, r + 7))
                    d = decay[:, r // 4].rearrange("p (c q) s -> p q c s", q=4)[:, r % 4]
                    stt(Ct[:, r % 2], R[r % 2][:, :].rearrange("p (c s) -> p c s", c=4), SC, d,
                        ALU.mult, ALU.mult).then_inc(c_d.sem, 1)
                for r in (r0, r0 + 1):
                    dve.wait_ge(c_hi.sem, c_hi.at(m, r + 1))
                    tt(Cs[1][:, r % 4], Ct[:, r % 2], Cs[0][:, r % 4], ALU.subtract).then_inc(c_lo.sem, 1)

            def center(m, b):
                hs = slice(b * NH, (b + 1) * NH)
                done = po_d[b]
                dve.wait_ge(av_s.sem, av_s.at(m, 2 * b + 2))
                dve.wait_ge(em_s.sem, em_s.at(m, 1))
                stt(st[:, 0, hs], u[:, hs, DH], -1.0, u[:, hs, DH], ALU.mult, ALU.max).then_inc(done.sem, 1)
                dve.wait_ge(done.sem, done.at(m, 1))
                tt(st[:, 1, hs], st[:, 0, hs], emt[:, hs], ALU.max).then_inc(done.sem, 1)
                dve.tensor_reduce(st[:, 3, hs], u[:, hs, 0:DH], AX, ALU.add).then_inc(done.sem, 1)
                dve.wait_ge(done.sem, done.at(m, 3))
                if b == 0 and past(m - 1):
                    dve.wait_ge(xt_p.sem, xt_p.at(m - 1, 2))
                stt(uc[:, b, :].rearrange("p (h e) -> p h e", e=DH), st[:, 3, hs].unsqueeze(2).to_broadcast([P, NH, DH]),
                    -1.0 / DH, u[:, hs, 0:DH], ALU.mult, ALU.add).then_inc(done.sem, 1)

            def spread(m, b):
                hs = slice(b * NH, (b + 1) * NH)
                done = po_d[b]
                dve.wait_ge(po_a[b].sem, po_a[b].at(m, 2))
                dve.tensor_reduce(st[:, 6, hs], u[:, hs, 0:DH], AX, ALU.add).then_inc(done.sem, 1)
                dve.wait_ge(done.sem, done.at(m, 5))
                stt(st[:, 4, hs], st[:, 6, hs], 1.0 / DH, st[:, 2, hs], ALU.mult, ALU.add).then_inc(done.sem, 1)
                tt(uc[:, b, :], uc[:, b, :], lnsg[:, :], ALU.mult).then_inc(done.sem, 1)

            def finish(m, b):
                done = po_d[b]
                dve.wait_ge(po_g[b].sem, po_g[b].at(m, 1))
                dve.wait_ge(done.sem, done.at(m, 7))
                v = uc[:, b, :].rearrange("p (h e) -> p h e", e=DH)
                tt(v, v, st[:, 5, b * NH:(b + 1) * NH].unsqueeze(2).to_broadcast([P, NH, DH]), ALU.mult)\
                    .then_inc(done.sem, 1)
                dve.wait_ge(done.sem, done.at(m, 8))
                tt(x1[:, b, :], uc[:, b, :], xres[:, b, :], ALU.add).then_inc(done.sem, 1)
                dve.wait_ge(done.sem, done.at(m, 9))
                dve.bn_stats(bn[:, 1, b, 0:6], x1[:, b, :]).then_inc(ln2.sem, 1)

            def router(n, tail):
                first, second = rt[:, 2:2 + 2 * NE], rt[:, 2 + 2 * NE:2 + 4 * NE]
                oh0 = first.rearrange("p (b e) -> p b e", b=2)
                oh1 = second.rearrange("p (b e) -> p b e", b=2)
                k = [20 if tail else 0]

                def step(ins, fence=True):
                    ins.then_inc(ro_d.sem, 1)
                    k[0] += 1
                    if fence:
                        dve.wait_ge(ro_d.sem, ro_d.at(n, k[0]))

                def be(i):
                    return mx[:, i, :].unsqueeze(2).to_broadcast([P, 2, NE])

                if tail:
                    dve.wait_ge(ro_e.sem, ro_e.at(n, 1))
                    step(dve.tensor_reduce(mx[:, 4, :], pe_[:, 0:2 * NE].rearrange("p (b e) -> p b e", b=2), AX, ALU.add))
                    step(dve.reciprocal(mx[:, 5, :], mx[:, 4, :]))
                    step(ts(rt[:, 0:2], mx[:, 5, :], tg[:, 1:2], None, ALU.mult), False)
                    step(stt(c2[:, :], pe_[:, 2 * NE:2 * NE + 2], 1.0, mx[:, 5, :], ALU.add, ALU.mult))
                    assert k[0] == ro_d.per
                    return
                ps = R[0][:, 0:2 * AC].rearrange("p (b k) -> p b k", b=2)
                dve.wait_ge(ro_p.sem, ro_p.at(n, 1))
                step(ts(u1s[:, :, :].rearrange("p (b e) r -> p b (e r)", b=2), ps[:, :, 0:R64], 1.0 / WS, None, ALU.mult), False)
                step(stt(lg[:, :, :], ps[:, :, R64:AC], 1.0 / WS, brb[:, :, :], ALU.mult, ALU.add))
                step(dve.tensor_reduce(mx[:, 0, :], lg[:, :, :], AX, ALU.max))
                step(tt(eq[:, :, :], lg[:, :, :], be(0), ALU.is_equal))
                step(tt(eq[:, :, :], eq[:, :, :], rev[:, :, :], ALU.mult))
                step(dve.tensor_reduce(mx[:, 1, :], eq[:, :, :], AX, ALU.max))
                step(tt(oh0, eq[:, :, :], be(1), ALU.is_equal))
                step(stt(l2[:, :, :], oh0, -1e30, lg[:, :, :], ALU.mult, ALU.add))
                step(dve.tensor_reduce(mx[:, 2, :], l2[:, :, :], AX, ALU.max))
                step(tt(eq[:, :, :], l2[:, :, :], be(2), ALU.is_equal), False)
                step(tt(ex[:, 0:2 * NE].rearrange("p (b e) -> p b e", b=2), lg[:, :, :], be(0), ALU.subtract), False)
                step(tt(ex[:, 2 * NE:2 * NE + 2], mx[:, 2, :], mx[:, 0, :], ALU.subtract))
                step(tt(eq[:, :, :], eq[:, :, :], rev[:, :, :], ALU.mult))
                step(dve.tensor_reduce(mx[:, 3, :], eq[:, :, :], AX, ALU.max))
                step(tt(oh1, eq[:, :, :], be(3), ALU.is_equal))
                step(tt(ohd[:, :, :], oh1, oh0, ALU.subtract))
                for i, oh in enumerate((first, ohd[:, :, :].rearrange("p b e -> p (b e)"))):
                    step(tt(zf[:, i], u1s[:, :, :], oh.unsqueeze(2).to_broadcast([P, 2 * NE, RK]), ALU.mult), i == 1)
                zfv = zf[:, :, :, :].rearrange("p i (b e) r -> p (i b) (e r)", b=2)
                step(dve.tensor_copy(zsp[:, :, 0, :], zfv))
                step(tt(zsp[:, :, 1, :], zfv, zsp[:, :, 0, :], ALU.subtract))
                assert k[0] == 20

            def weights(j):
                done = sum(parts[:j])
                for i, (c0, c1_, s, dst) in enumerate(jobs[j][1]):
                    dve.wait_ge(w_hi.sem, done + i + 1)
                    stt(dst[1], staged(j, c0, c1_, dst), s, dst[0], ALU.mult, ALU.subtract).then_inc(w_lo.sem, 1)

            def body(t):
                u_, m, p = t - 1, t + 1, t + 2
                for i in range(NS):
                    if i == 1 and ok(u_):
                        dve.wait_ge(w2_p.sem, w2_p.at(u_, NS))
                        uu = U[:, :].rearrange("p (w x r) -> p w x r", w=4, x=2)
                        flat = "p (b e) r -> p b (e r)"
                        wide = "p w (b e) r -> p (w b) (e r)"
                        bce = [rtk[:, 2 + 2 * NE * c:2 + 2 * NE * (c + 1)].unsqueeze(2).to_broadcast([P, 2 * NE, RK])
                               for c in range(2)]
                        ts(uv[:, 2:4].rearrange(wide, b=2), uu[:, :, 1, :], 1.0 / WS, None, ALU.mult)\
                            .then_inc(z2_d.sem, 1)
                        dve.wait_ge(z2_d.sem, z2_d.at(u_, 1))
                        stt(uv[:, 0:2].rearrange(wide, b=2), uu[:, :, 0, :], 1.0 / WS,
                            uv[:, 2:4].rearrange(wide, b=2), ALU.mult, ALU.add).then_inc(z2_d.sem, 1)
                        dve.wait_ge(z2_d.sem, z2_d.at(u_, 2))
                        tt(uv[:, 0], uv[:, 0], uv[:, 1], ALU.subtract).then_inc(z2_d.sem, 1)
                        tt(uv[:, 2], uv[:, 1], bce[1], ALU.mult).then_inc(z2_d.sem, 1)
                        dve.wait_ge(z2_d.sem, z2_d.at(u_, 3))
                        tt(uv[:, 3], uv[:, 0], bce[0], ALU.mult).then_inc(z2_d.sem, 1)
                        dve.wait_ge(z2_d.sem, z2_d.at(u_, 5))
                        tt(uv[:, 1], uv[:, 2], uv[:, 3], ALU.add).then_inc(z2_d.sem, 1)
                        dve.wait_ge(z2_d.sem, z2_d.at(u_, 6))
                        dve.tensor_copy(z2sp[:, :, 0, :], uv[:, 1].rearrange(flat, b=2)).then_inc(z2_d.sem, 1)
                        dve.wait_ge(z2_d.sem, z2_d.at(u_, 7))
                        tt(z2sp[:, :, 1, :], uv[:, 1].rearrange(flat, b=2), z2sp[:, :, 0, :], ALU.subtract)\
                            .then_inc(z2_d.sem, 1)
                    if i == 2 and ok(u_):
                        dve.wait_ge(y_p.sem, y_p.at(u_, 1))
                        if past(u_ - 1):
                            dve.wait_ge(st_o.sem, st_o.at(u_ - 1, 16))
                        for b in range(2):
                            stt(xoo[:, 2 + b, :], Y[b][:, :], rtk[:, b:b + 1], xoo[:, b, :], ALU.mult, ALU.add)\
                                .then_inc(y_d.sem, 1)
                    if i == 2 and ok(t):
                        if past(t - 1):
                            dve.wait_ge(y_d.sem, y_d.at(t - 1, 2))
                        dve.tensor_copy(rtk[:, :], rt[:, :]).then_inc(xo_d.sem, 1)
                        for b in range(2):
                            stt(xoo[:, b, :], b2g[:, :], c2[:, b:b + 1], x1[:, b, :], ALU.mult, ALU.add)\
                                .then_inc(xo_d.sem, 1)
                    if i == 2 and ok(p):
                        dve.wait_ge(ld_x.sem, ld_x.at(p, 16))
                        for b in range(2):
                            dve.bn_stats(bn[:, 0, b, 0:6], xin[:, b, :]).then_inc(ln1.sem, 1)
                        dve.wait_ge(ln1.sem, ln1.at(p, 2))
                        if past(p - 1):
                            dve.wait_ge(rs1.sem, rs1.at(p - 1, 2))
                        apart(dve, p - 1, passed)
                        dve.bn_aggr(bn[:, 0, 0, 6:8], bn[:, 0, 0, 0:6])
                        dve.bn_aggr(bn[:, 0, 1, 6:8], bn[:, 0, 1, 0:6]).then_inc(ln1.sem, 1)
                    if i in (3, 4) and ok(m):
                        decayed(m, 4 * (i - 3))
                    if i == 4 and ok(m):
                        center(m, 0)
                        decayed(m, 6)
                    if i == 6 and ok(m):
                        finish(m, 0)
                    if i == 5 and ok(m):
                        spread(m, 0)
                        center(m, 1)
                    if i == 7 and ok(m):
                        dve.wait_ge(rs2.sem, rs2.at(m, 2))
                        for b in range(2):
                            ts(uc[:, b, :], x1[:, b, :], bn[:, 1, b, 6:7], rv[:, 1, 1, b:b + 1], ALU.subtract, ALU.mult)\
                                .then_inc(xn_d.sem, 1)
                    if i == 0:
                        if ok(u_):
                            combine(u_, NS - 1)
                        if ok(m):
                            dve.wait_ge(lf_p.sem, lf_p.at(m, 1))
                            dve.tensor_copy(aT[:, :], G[0:HB, 64:192]).then_inc(mx_d.sem, 1)
                            dve.wait_ge(mx_d.sem, mx_d.at(m, 1))
                            if past(m - 1):
                                dve.wait_ge(m_wr.sem, m_wr.at(m - 1, 16))
                            dve.tensor_tensor_scan(MT[:, :], aT[:, :], aT[:, :], -3.0e38, ALU.max, ALU.max)\
                                .then_inc(mx_d.sem, 1)
                            dve.wait_ge(mx_d.sem, mx_d.at(m, 2))
                            if past(m - 1):
                                dve.wait_ge(em_a.sem, em_a.at(m - 1, 1))
                            tt(FM[:, :], G[0:HB, 192:320], MT[:, :], ALU.add).then_inc(mx_d.sem, 1)
                            if past(m - 1):
                                dve.wait_ge(arg_g.sem, arg_g.at(m - 1, 4))
                            tt(acol[:, :], G[:, 320:352], gb[:, 0:HB], ALU.add).then_inc(mx_d.sem, 1)
                        if ok(t):
                            if isinstance(t, int) and t == 0:
                                dve.wait_ge(c_pool.sem, 11 + NE)
                            router(t, False)
                            router(t, True)
                    elif ok(t):
                        combine(t, i - 1)
                    if i == 3 and ok(m):
                        decayed(m, 2)
                    if i == 3 and ok(p):
                        dve.wait_ge(rs1.sem, rs1.at(p, 2))
                        for b in range(2):
                            ts(qn[:, b, :], xin[:, b, :], bn[:, 0, b, 6:7], rv[:, 0, 1, b:b + 1], ALU.subtract, ALU.mult)\
                                .then_inc(q_nd.sem, 1)
                    if i == 5 and ok(m):
                        spread(m, 1)
                    if i == 5 and ok(p):
                        for b in range(2):
                            dve.wait_ge(qt_h.sem, qt_h.at(p, b + 1))
                            tt(qT[1][:, :, b, :], R[b][:, :].rearrange("p (c s) -> p c s", c=DC), qT[0][:, :, b, :],
                               ALU.subtract).then_inc(qt_l.sem, 1)
                    if i == 6 and ok(p):
                        dve.wait_ge(gat_p.sem, gat_p.at(p, 1))
                        stt(gb[:, :], G[:, 0:4 * NH], 1.0 / WS, bg[:, :], ALU.mult, ALU.add).then_inc(gat_s.sem, 1)
                        dve.wait_ge(gat_s.sem, gat_s.at(p, 1))
                        stt(gt[:, 0, :], gb[:, HB:], -1.0, gb[:, HB:], ALU.mult, ALU.min).then_inc(gat_s.sem, 1)
                    if i == 6 and ok(m):
                        finish(m, 1)
                        dve.wait_ge(ln2.sem, ln2.at(m, 2))
                        apart(dve, m, passed)
                        dve.bn_aggr(bn[:, 1, 0, 6:8], bn[:, 1, 0, 0:6])
                        dve.bn_aggr(bn[:, 1, 1, 6:8], bn[:, 1, 1, 0:6]).then_inc(ln2.sem, 1)
                    if i == 6 and ok(p):
                        dve.wait_ge(gat_e.sem, gat_e.at(p, 2))
                        stt(gt[:, 3, :], gb[:, HB:], 0.0, gt[:, 2, :], ALU.min, ALU.subtract).then_inc(lf_d.sem, 1)
                    if isinstance(t, int) and t == -2 and i == 4:
                        dve.wait_ge(c_act.sem, 1)
                        ts(lnsg[:, :], lnsg[:, :], tg[:, 2:3], None, ALU.mult).then_inc(c_dve.sem, 1)
                        ts(b2g[:, :], b2g[:, :], tg[:, 3:4], None, ALU.mult).then_inc(c_dve.sem, 1)
                        ts(tg[:, 1:2], tg[:, 3:4], 1.0 / WS, None, ALU.mult).then_inc(c_dve.sem, 1)
                        tt(wg[:, DC:2 * DC, :], wg[:, DC:2 * DC, :], wg[:, 2 * DC:3 * DC, :], ALU.add).then_inc(c_dve.sem, 1)
                        dve.wait_ge(c_dve.sem, 4)
                        ts(wgs[0][:, :, :], wg[:, 0:2 * DC, :], WS, None, ALU.mult).then_inc(c_dve.sem, 1)
                        dve.wait_ge(c_dve.sem, 5)
                        stt(wgs[1][:, :, :], wg[:, 0:2 * DC, :], WS, wgs[0][:, :, :], ALU.mult, ALU.subtract)\
                            .then_inc(c_dve.sem, 1)
                    if isinstance(t, int) and t < 0:
                        for j in WSLOT.get((t, i), ()):
                            weights(j)
                if ok(m):
                    for b in range(2):
                        dve.wait_ge(xt_h.sem, xt_h.at(m, b + 1))
                        sl = slice(b * P, (b + 1) * P)
                        tt(xT[1][:, :, sl], R[b][:, :].rearrange("p (c s) -> p c s", c=DC), xT[0][:, :, sl],
                           ALU.subtract).then_inc(xt_l.sem, 1)
            steps(dve, body)

        @block.tensor
        def _(pe):
            def mm(out_, l, r, start, stop=False):
                return pe.matmul(out_, l, r, start=start, stop=stop, skip_group_check=True)

            def base(n, i):
                prior = (n, i - 2) if i >= 2 else (n - 1, i - 2 + NS)
                if past(prior[0]):
                    pe.wait_ge(g1_a.sem, g1_a.at(prior[0], 2 * prior[1] + 2))
                for k in range(2):
                    f = 2 * i + k
                    for c in range(DC):
                        for a, b in ((0, 0), (0, 1), (1, 0)):
                            mm(H[i % 2][:, k * T:(k + 1) * T], w1[a][:, c, f * P:(f + 1) * P], xT[b][:, c, :],
                               start=(k == 0 and c == 0 and a == 0 and b == 0))

            def lora(n, i, which, done):
                for k in range(2):
                    f = 2 * i + k
                    for a in range(2):
                        last = mm(H[i % 2][:, k * T:(k + 1) * T], b1w[a][:, f * P:(f + 1) * P], zs[:, which, :],
                                  start=False, stop=(a == 1))
                last.then_inc(done.sem, 1)

            def delta(n, i):
                pe.wait_ge(g0_a.sem, g0_a.at(n, 2 * i + 2))
                lora(n, i, 1, del_p)

            def lora2(i, k, b, what):
                f = 2 * i + k
                tok = slice(k * T + b * P, k * T + (b + 1) * P)
                o = (2 * what + b) * 2 * R64
                for a, w in ((0, 0), (0, 1), (1, 0)):
                    l = gv[a][:, i % 2, what, tok]
                    if w == 0:
                        last = mm(U[:, o:o + (2 - a) * R64], l, a2[:, f, 0:2 - a, :].rearrange("p a r -> p (a r)"),
                                  start=(what == 1 and i == 0 and k == 0 and b == 0 and a == 0))
                    if what == 0:
                        last = mm(Y[b][:, :], l, w2[w][:, f, :], start=(i == 0 and k == 0 and a == 0 and w == 0))
                return last

            def piece(i, k, b):
                lora2(i, k, b, 1)
                return lora2(i, k, b, 0)

            def second(n, i):
                pe.wait_ge(lo_d.sem, lo_d.at(n, 2 * i + 1))
                for k in range(2):
                    for b in range(2):
                        lora2(i, k, b, 1)
                pe.wait_ge(lo_d.sem, lo_d.at(n, 2 * i + 2))
                if i == 0 and past(n - 1):
                    pe.wait_ge(y_d.sem, y_d.at(n - 1, 2))
                for k in range(2):
                    for b in range(2):
                        last = lora2(i, k, b, 0)
                last.then_inc(w2_p.sem, 1)

            def body(t):
                u_, m, p = t - 1, t + 1, t + 2
                if isinstance(t, int) and t == -2:
                    pe.wait_ge(c_pool.sem, 11 + NE)
                if isinstance(t, int) and t == 0:
                    pe.wait_ge(w_hi.sem, sum(parts[:-1]))
                    pe.wait_ge(w_lo.sem, sum(parts[:-1]))
                for i in range(NS):
                    if ok(t) and i > 1:
                        base(t, i)
                        lora(t, i, 0, base_p)
                    if i == 2 and ok(u_):
                        pe.wait_ge(z2_d.sem, z2_d.at(u_, 8))
                        for b in range(2):
                            last = pe.transpose(R[0][:, b * R64:(b + 1) * R64].bitcast(F16)[:, 0:P],
                                                z2sp[:, b].rearrange("p a r -> p (a r)"), identh[:, :])
                        last.then_inc(z2_p.sem, 1)
                    if i == 3 and ok(m):
                        pe.wait_ge(em_a.sem, em_a.at(m, 1))
                        apart(pe, m, passed)
                        pe.transpose(G[:, 480:512], em[:, :], ident[0:HB, 0:HB]).then_inc(em_p.sem, 1)
                    if i == 4 and ok(m):
                        products(m, 0)
                        scores(m, 4, t)
                    if i == 0:
                        if ok(u_):
                            delta(u_, NS - 1)
                        if ok(m):
                            pe.wait_ge(lf_d.sem, lf_d.at(m, 1))
                            lf = gt[:, 3, :]
                            mm(G[:, 320:352], ntri[:, :], lf, True, True)
                            mm(G[0:HB, 64:192], gb[:, 0:HB], ident[:, :], True)
                            mm(G[0:HB, 64:192], lf, ntri[:, :], False, True)
                            mm(G[0:HB, 192:320], lf, tri[:, :], True, True).then_inc(lf_p.sem, 1)
                        if ok(u_):
                            second(u_, NS - 2)
                        if ok(t):
                            pe.wait_ge(xt_l.sem, xt_l.at(t, 2))
                            for b in range(2):
                                for c in range(DC):
                                    for a, w in ((0, 0), (0, 1), (1, 0)):
                                        last = mm(R[0][:, b * AC:(b + 1) * AC], xT[a][:, c, b * P:(b + 1) * P],
                                                  a1[w][:, c, :], start=(c == 0 and a == 0 and w == 0),
                                                  stop=(c == DC - 1 and a == 1))
                            last.then_inc(ro_p.sem, 1)
                            base(t, 0)
                            base(t, 1)
                        if ok(u_):
                            pe.wait_ge(lo_d.sem, lo_d.at(u_, 2 * NS))
                            piece(NS - 1, 0, 0)
                        if ok(t):
                            pe.wait_ge(ro_d.sem, ro_d.at(t, 20))
                            for j in range(4):
                                last = pe.transpose(R[1][:, j * R64:(j + 1) * R64].bitcast(F16)[:, 0:P],
                                                    zsp[:, j].rearrange("p a r -> p (a r)"), identh[:, :])
                            last.then_inc(z_p.sem, 1)
                        if ok(u_):
                            piece(NS - 1, 0, 1)
                        if ok(t):
                            pe.wait_ge(z_s.sem, z_s.at(t, 1))
                            if isinstance(t, int) and t == 0:
                                pe.wait_ge(w_hi.sem, sum(parts))
                                pe.wait_ge(w_lo.sem, sum(parts))
                            lora(t, 0, 0, base_p)
                            lora(t, 1, 0, base_p)
                            pe.wait_ge(ro_e.sem, ro_e.at(t, 1))
                            for b in range(2):
                                last = pe.transpose(R[1][:, T + b * P:T + (b + 1) * P],
                                                    pe_[:, 2 * NE + b:2 * NE + b + 1].to_broadcast([P, P]), ident[:, :])
                            last.then_inc(z_p.sem, 1)
                        if ok(u_):
                            piece(NS - 1, 1, 0)
                    elif i == 1:
                        if ok(t):
                            delta(t, 0)
                        if ok(u_):
                            piece(NS - 1, 1, 1).then_inc(w2_p.sem, 1)
                    else:
                        if ok(t):
                            delta(t, i - 1)
                        if i == 2 and ok(u_):
                            pe.wait_ge(z2_s.sem, z2_s.at(u_, 1))
                            for b in range(2):
                                for a in range(2):
                                    last = mm(Y[b][:, :], z2s[:, b, :], b2w[a][:, :], start=False, stop=(a == 1))
                            last.then_inc(y_p.sem, 1)
                        if i == 4 and ok(m):
                            products(m, 1)
                        if i == 5 and ok(m):
                            products(m, 3)
                        if i == 5 and ok(p):
                            for b in range(2):
                                pe.wait_ge(q_nd.sem, q_nd.at(p, b + 1))
                                if ok(m):
                                    pe.wait_ge(c_d.sem, c_d.at(m, 7 + b))
                                for c in range(DC):
                                    last = pe.transpose(R[b][:, c * P:(c + 1) * P], qn[:, b, c * P:(c + 1) * P], ident[:, :])
                                last.then_inc(qt_p.sem, 1)
                        if i == 2 and ok(m):
                            scores(m, 0, t)
                        if ok(t):
                            second(t, i - 2)
                        if i == 6 and ok(p):
                            if ok(m):
                                pe.wait_ge(av_s.sem, av_s.at(m, 4))
                            if isinstance(t, int) and t == -2:
                                pe.wait_ge(c_dve.sem, 6)
                            pe.wait_ge(cp_k.sem, cp_k.at(p, 2))
                            pe.wait_ge(qt_l.sem, qt_l.at(p, 2))
                            for b in range(2):
                                o = G[:, 0:4 * NH].rearrange("p (k b h) -> p k b h", k=2, b=2)[:, :, b, :]
                                for c in range(2 * DC):
                                    for a, w in ((0, 0), (0, 1), (1, 0)):
                                        l = qT[a][:, c, b, :] if c < DC else kT[a][:, c - DC, b * P:(b + 1) * P]
                                        last = mm(o, l, wgs[w][:, c, :].rearrange("p (k h) -> p k h", k=2),
                                                  start=(c == 0 and a == 0 and w == 0), stop=(c == 2 * DC - 1 and a == 1))
                            last.then_inc(gat_p.sem, 1)
                        if i == 7 and ok(m):
                            for b in range(2):
                                pe.wait_ge(xn_d.sem, xn_d.at(m, b + 1))
                                if ok(p):
                                    pe.wait_ge(qt_l.sem, qt_l.at(p, b + 1))
                                for c in range(DC):
                                    last = pe.transpose(R[b][:, c * P:(c + 1) * P], uc[:, b, c * P:(c + 1) * P], ident[:, :])
                                last.then_inc(xt_p.sem, 1)
                    if i == 3 and ok(m):
                        scores(m, 2, t)
                    if i == 4 and ok(m):
                        scores(m, 6, t)
                        products(m, 2)
            def scores(m, r0, t):
                for r in (r0, r0 + 1):
                    if r >= 2:
                        pe.wait_ge(c_d.sem, c_d.at(m, r - 1))
                    elif ok(t):
                        pe.wait_ge(ro_d.sem, ro_d.at(t, 2))
                        pe.wait_ge(z_s.sem, z_s.at(t, 2))
                    q, b = r % 4, r // 4
                    rows = slice(DH * q, DH * (q + 1))
                    for c in range(DC):
                        for a, w in ((0, 0), (0, 1), (1, 0)):
                            last = mm(R[r % 2][:, c * P:(c + 1) * P], kT[a][rows, c, b * P:(b + 1) * P],
                                      qT[w][rows, c, b, :], start=(a == 0 and w == 0), stop=(a == 1))
                    last.then_inc(qk_p.sem, 1)

            def products(m, g):
                if g == 0:
                    pe.wait_ge(em_s.sem, em_s.at(m, 1))
                    pe.wait_ge(cp_v.sem, cp_v.at(m, 2))
                else:
                    pe.wait_ge(av_s.sem, av_s.at(m, g))
                for r in (2 * g, 2 * g + 1):
                    pe.wait_ge(c_lo.sem, c_lo.at(m, r + 1))
                    for c in range(4):
                        o = ((r % 2) * 4 + c) * (DH + 1)
                        for a, w in ((0, 0), (0, 1), (1, 0)):
                            last = mm(G[:, o:o + DH + 1], Cs[a][:, r % 4, c, :], vaug[w][:, r // 4, 4 * c + r % 4, :],
                                      start=(a == 0 and w == 0), stop=(a == 1))
                last.then_inc(av_p.sem, 1)
            steps(pe, body)


def kernel(x, ctx_2048, g_xattn, g_ffn, L0_xattn_Wi, L0_xattn_bi, L0_xattn_Wf, L0_xattn_bf, L0_xattn_ln_scale,
           L0_ffn_W_r, L0_ffn_b_r, L0_ffn_W1, L0_ffn_b1, L0_ffn_W2, L0_ffn_b2, L0_ffn_A1, L0_ffn_B1, L0_ffn_A2,
           L0_ffn_B2):
    import numpy as np
    import concourse.bacc as bacc
    from concourse import mybir as mb
    from concourse.bass_utils import run_bass_kernel_spmd as run

    A = np.asarray
    nb, s, d = A(x).shape
    e, f, r = A(L0_ffn_B1).shape
    ctx = A(ctx_2048)
    wgate = np.concatenate([A(L0_xattn_Wi), A(L0_xattn_Wf)], axis=1)
    arrays = {
        "x": A(x),
        "ctx_tok": ctx,
        "ctx_T": ctx.reshape(nb // 2, 2 * s, d).transpose(0, 2, 1),
        "gx": A(g_xattn), "gf": A(g_ffn),
        "wgate": wgate.reshape(-1, 128, wgate.shape[1]).transpose(1, 0, 2),
        "bgate": np.concatenate([A(L0_xattn_bi)] * 2 + [A(L0_xattn_bf)] * 2),
        "lnscale": A(L0_xattn_ln_scale),
        "w1t": A(L0_ffn_W1).T, "w2t": A(L0_ffn_W2).T,
        "b1c": A(L0_ffn_b1).reshape(-1, 128).T, "b2": A(L0_ffn_b2),
        "a1r": np.concatenate([A(L0_ffn_A1).reshape(e * r, d).T, A(L0_ffn_W_r).T], axis=1),
        "br": A(L0_ffn_b_r),
        "b1lo": A(L0_ffn_B1).transpose(0, 2, 1).reshape(e * r, f),
        "a2t": A(L0_ffn_A2).reshape(e * r, f).T,
        "b2lo": A(L0_ffn_B2).transpose(0, 2, 1).reshape(e * r, d),
    }
    nc = bacc.Bacc("TRN2", target_bir_lowering=False, num_devices=1)
    ins, args = {}, []
    for name, a in arrays.items():
        a = np.ascontiguousarray(a)
        ins["in_" + name] = a
        args.append(nc.dram_tensor("in_" + name, a.shape, mb.dt.from_np(a.dtype), kind="ExternalInput").ap())
    args.append(nc.dram_tensor("out_0", A(x).shape, mb.dt.float32, kind="ExternalOutput").ap())
    flamingo_kernel(nc, *args)
    res = run(nc, [ins], core_ids=[0])
    return res.results[0]["out_0"]
```
